# Optimizing a Trainium2 kernel written in Bass

```python
import numpy as np
import jax
import jax.numpy as jnp

def _softmax(x, axis=-1):
    return jax.nn.softmax(x, axis=axis)

def _gelu(x):
    return jax.nn.gelu(x, approximate=True)

def _silu(x):
    return jax.nn.silu(x)

def _sigmoid(x):
    return jax.nn.sigmoid(x)

def _layernorm(x, axis=-1, eps=1e-05):
    m = jnp.mean(x, axis=axis, keepdims=True)
    v = jnp.var(x, axis=axis, keepdims=True)
    return (x - m) / jnp.sqrt(v + eps)

def _scatter_add(tgt, idx, src, axis=0):
    return tgt.at[idx].add(src)

def _segment_sum(src, seg, n):
    return jax.ops.segment_sum(src, seg, n)
kernel_name = 'mk_gnn_preln_d1_gnn_r8_3833f6'

def setup_inputs(seed: int=0):
    np.random.seed(seed)
    _w = jnp.asarray

    def _rec_inputs():
        import jax
        import jax.numpy as jnp
        _gk = jax.random.key(seed)
        x = -0.000202 + 1 * jax.random.normal(jax.random.fold_in(_gk, 1), (12500, 160), jnp.float32)
        src = jax.random.randint(jax.random.fold_in(_gk, 2), (200000,), 0, 12500, jnp.int32)
        dst = jnp.minimum((12500 * jax.random.uniform(jax.random.fold_in(_gk, 3), (200000,)) ** 2.0).astype(jnp.int32), 99999)
        _o = jnp.argsort(dst, stable=True)
        src = src[_o]
        dst = dst[_o]
        edge_attr_4 = 0.0012443 + 1.0001 * jax.random.normal(jax.random.fold_in(_gk, 12), (200000, 4), jnp.float32)
        edge_attr_64 = 0.000127647 + 1.00004 * jax.random.normal(jax.random.fold_in(_gk, 13), (200000, 64), jnp.float32)
        node_vec1 = jax.random.uniform(jax.random.fold_in(_gk, 14), (12500, 1), jnp.float32, 0.0, 1)
        return (x, src, dst, edge_attr_4, edge_attr_64, node_vec1)
    x, src, dst, edge_attr_4, edge_attr_64, node_vec1 = _rec_inputs()

    def _L0_gnn_setup():
        import jax, jax.numpy as jnp
        import numpy as np
        N, E = (5000, 80000)
        S_IN, V_IN = (64, 32)
        S_MID, V_MID = (96, 128)
        S_OUT, V_OUT = (96, 32)
        R = 64
        FC_HID = 64
        W_NUMEL = 64 + 64 + 32 + 32 + 32
        NUM_NEIGHBORS = 16.0

        def _inv(d):
            return 1.0 / jnp.sqrt(jnp.float32(d))

        def _forward(node_features, node_attr, edge_attr, edge_scalars, lin1_ws, lin1_wv, fc_w1, fc_w2, sc_ws, sc_wv, lin2_ws, lin2_wv, edge_src, edge_dst):
            n = node_features.shape[0]
            s = node_features[:, :S_IN]
            v = node_features[:, S_IN:].reshape(n, V_IN, 3)
            a = node_attr
            sc_s = s @ sc_ws * a * _inv(S_IN)
            sc_v = jnp.einsum('nci,cd->ndi', v, sc_wv) * a[:, :, None] * _inv(V_IN)
            h_s = s @ lin1_ws * a * _inv(S_IN)
            h_v = jnp.einsum('nci,cd->ndi', v, lin1_wv) * a[:, :, None] * _inv(V_IN)
            hid = jax.nn.silu(edge_scalars @ fc_w1 * _inv(R))
            w = hid @ fc_w2 * _inv(FC_HID)
            w1, w2, w3, w4, w5 = jnp.split(w, [64, 128, 160, 192], axis=-1)
            es = h_s[edge_src]
            ev = h_v[edge_src]
            e0 = edge_attr[:, :1]
            e1 = edge_attr[:, 1:4]
            m_s1 = w1 * es * e0
            m_s2 = w4 * jnp.einsum('eci,ei->ec', ev, e1) * _inv(3)
            m_v1 = (w2 * es)[:, :, None] * e1[:, None, :]
            m_v2 = w3[:, :, None] * ev * e0[:, :, None]
            m_v3 = w5[:, :, None] * jnp.cross(ev, e1[:, None, :]) * _inv(2)
            mid_s = jnp.concatenate([m_s1, m_s2], axis=-1)
            mid_v = jnp.concatenate([m_v1, m_v2, m_v3], axis=1)
            inv_nn = 1.0 / jnp.sqrt(jnp.float32(NUM_NEIGHBORS))
            agg_s = jax.ops.segment_sum(mid_s, edge_dst, num_segments=n) * inv_nn
            agg_v = jax.ops.segment_sum(mid_v, edge_dst, num_segments=n) * inv_nn
            o_s = agg_s @ lin2_ws * a * _inv(S_MID)
            o_v = jnp.einsum('nci,cd->ndi', agg_v, lin2_wv) * a[:, :, None] * _inv(V_MID)
            pre_s = sc_s + o_s
            pre_v = sc_v + o_v
            scalars = jax.nn.silu(pre_s[:, :64])
            gates = jax.nn.sigmoid(pre_s[:, 64:96])
            gated = gates[:, :, None] * pre_v
            return jnp.concatenate([scalars, gated.reshape(n, 3 * V_OUT)], axis=-1)
        key = jax.random.key(seed)
        ks = jax.random.split(key, 13)
        return {'node_features': jax.random.normal(ks[0], (N, S_IN + 3 * V_IN), jnp.float32), 'node_attr': jnp.ones((N, 1), jnp.float32), 'edge_src': jax.random.randint(ks[1], (E,), 0, N), 'edge_dst': jax.random.randint(ks[2], (E,), 0, N), 'edge_attr': jax.random.normal(ks[3], (E, 4), jnp.float32), 'edge_scalars': jax.random.normal(ks[4], (E, R), jnp.float32), 'lin1_ws': jax.random.normal(ks[5], (S_IN, S_IN), jnp.float32), 'lin1_wv': jax.random.normal(ks[6], (V_IN, V_IN), jnp.float32), 'fc_w1': jax.random.normal(ks[7], (R, FC_HID), jnp.float32), 'fc_w2': jax.random.normal(ks[8], (FC_HID, W_NUMEL), jnp.float32), 'sc_ws': jax.random.normal(ks[9], (S_IN, S_OUT), jnp.float32), 'sc_wv': jax.random.normal(ks[10], (V_IN, V_OUT), jnp.float32), 'lin2_ws': jax.random.normal(ks[11], (S_MID, S_OUT), jnp.float32), 'lin2_wv': jax.random.normal(ks[12], (V_MID, V_OUT), jnp.float32)}
    _L0_gnn_all = _L0_gnn_setup()
    _L0_gnn_in = {k: v for k, v in _L0_gnn_all.items() if k in ('lin1_ws', 'lin1_wv', 'fc_w1', 'fc_w2', 'sc_ws', 'sc_wv', 'lin2_ws', 'lin2_wv')}
    del _L0_gnn_all
    return {'x': x, 'src': src, 'dst': dst, 'edge_attr_4': edge_attr_4, 'edge_attr_64': edge_attr_64, 'node_vec1': node_vec1, 'L0_gnn_lin1_ws': _L0_gnn_in['lin1_ws'], 'L0_gnn_lin1_wv': _L0_gnn_in['lin1_wv'], 'L0_gnn_fc_w1': _L0_gnn_in['fc_w1'], 'L0_gnn_fc_w2': _L0_gnn_in['fc_w2'], 'L0_gnn_sc_ws': _L0_gnn_in['sc_ws'], 'L0_gnn_sc_wv': _L0_gnn_in['sc_wv'], 'L0_gnn_lin2_ws': _L0_gnn_in['lin2_ws'], 'L0_gnn_lin2_wv': _L0_gnn_in['lin2_wv']}

def reference(x, src, dst, edge_attr_4, edge_attr_64, node_vec1, L0_gnn_lin1_ws, L0_gnn_lin1_wv, L0_gnn_fc_w1, L0_gnn_fc_w2, L0_gnn_sc_ws, L0_gnn_sc_wv, L0_gnn_lin2_ws, L0_gnn_lin2_wv):
    import jax
    import jax.numpy as jnp

    def _L0_gnn_ref(node_features, node_attr, edge_src, edge_dst, edge_attr, edge_scalars, lin1_ws, lin1_wv, fc_w1, fc_w2, sc_ws, sc_wv, lin2_ws, lin2_wv):
        import jax, jax.numpy as jnp
        import numpy as np
        N, E = (5000, 80000)
        S_IN, V_IN = (64, 32)
        S_MID, V_MID = (96, 128)
        S_OUT, V_OUT = (96, 32)
        R = 64
        FC_HID = 64
        W_NUMEL = 64 + 64 + 32 + 32 + 32
        NUM_NEIGHBORS = 16.0

        def _inv(d):
            return 1.0 / jnp.sqrt(jnp.float32(d))

        def _forward(node_features, node_attr, edge_attr, edge_scalars, lin1_ws, lin1_wv, fc_w1, fc_w2, sc_ws, sc_wv, lin2_ws, lin2_wv, edge_src, edge_dst):
            n = node_features.shape[0]
            s = node_features[:, :S_IN]
            v = node_features[:, S_IN:].reshape(n, V_IN, 3)
            a = node_attr
            sc_s = s @ sc_ws * a * _inv(S_IN)
            sc_v = jnp.einsum('nci,cd->ndi', v, sc_wv) * a[:, :, None] * _inv(V_IN)
            h_s = s @ lin1_ws * a * _inv(S_IN)
            h_v = jnp.einsum('nci,cd->ndi', v, lin1_wv) * a[:, :, None] * _inv(V_IN)
            hid = jax.nn.silu(edge_scalars @ fc_w1 * _inv(R))
            w = hid @ fc_w2 * _inv(FC_HID)
            w1, w2, w3, w4, w5 = jnp.split(w, [64, 128, 160, 192], axis=-1)
            es = h_s[edge_src]
            ev = h_v[edge_src]
            e0 = edge_attr[:, :1]
            e1 = edge_attr[:, 1:4]
            m_s1 = w1 * es * e0
            m_s2 = w4 * jnp.einsum('eci,ei->ec', ev, e1) * _inv(3)
            m_v1 = (w2 * es)[:, :, None] * e1[:, None, :]
            m_v2 = w3[:, :, None] * ev * e0[:, :, None]
            m_v3 = w5[:, :, None] * jnp.cross(ev, e1[:, None, :]) * _inv(2)
            mid_s = jnp.concatenate([m_s1, m_s2], axis=-1)
            mid_v = jnp.concatenate([m_v1, m_v2, m_v3], axis=1)
            inv_nn = 1.0 / jnp.sqrt(jnp.float32(NUM_NEIGHBORS))
            agg_s = jax.ops.segment_sum(mid_s, edge_dst, num_segments=n) * inv_nn
            agg_v = jax.ops.segment_sum(mid_v, edge_dst, num_segments=n) * inv_nn
            o_s = agg_s @ lin2_ws * a * _inv(S_MID)
            o_v = jnp.einsum('nci,cd->ndi', agg_v, lin2_wv) * a[:, :, None] * _inv(V_MID)
            pre_s = sc_s + o_s
            pre_v = sc_v + o_v
            scalars = jax.nn.silu(pre_s[:, :64])
            gates = jax.nn.sigmoid(pre_s[:, 64:96])
            gated = gates[:, :, None] * pre_v
            return jnp.concatenate([scalars, gated.reshape(n, 3 * V_OUT)], axis=-1)
        return _forward(node_features, node_attr, edge_attr, edge_scalars, lin1_ws, lin1_wv, fc_w1, fc_w2, sc_ws, sc_wv, lin2_ws, lin2_wv, edge_src, edge_dst)
    h = jnp.maximum(_layernorm(x, axis=-1), 0.0)
    x = x + _L0_gnn_ref(h, node_vec1, src, dst, edge_attr_4, edge_attr_64, L0_gnn_lin1_ws, L0_gnn_lin1_wv, L0_gnn_fc_w1, L0_gnn_fc_w2, L0_gnn_sc_ws, L0_gnn_sc_wv, L0_gnn_lin2_ws, L0_gnn_lin2_wv)
    return x

_drawn_inputs = setup_inputs


def setup_inputs(seed=0):
    import zlib

    import numpy as np

    out = dict(_drawn_inputs(seed))
    spreads = {}
    factors = {}
    for name, (base, spread) in spreads.items():
        noise = np.random.default_rng([zlib.crc32(name.encode()), seed]).standard_normal(out[name].shape)
        drawn = base * np.exp(spread * noise) if base else spread * noise
        out[name] = jnp.asarray(drawn.astype(out[name].dtype))
    for name, factor in factors.items():
        out[name] = (out[name] * factor).astype(out[name].dtype)
    return out
```

```python
import math
from contextlib import ExitStack

import concourse.bass as bass
from concourse import mybir

F32 = mybir.dt.float32
I32 = mybir.dt.int32
ALU = mybir.AluOpType
ACT = mybir.ActivationFunctionType
AX = mybir.AxisListType

P = 128
NODES, EDGES, FEAT = 12500, 200000, 160
NS, NV, HID, WNUM = 64, 32, 64, 224
VEC = 3 * NV
OUTS = 96

NODE_TILES = -(-NODES // P)
NODES_PAD = NODE_TILES * P
GROUP = 7
NODE_ITERS = NODE_TILES // (2 * GROUP)
assert NODE_ITERS * 2 * GROUP == NODE_TILES

TILES_W = 3
SLOTS = 64
STEP_TILES = 2 * TILES_W
PAIRS = STEP_TILES // 2
STEPS = -(-EDGES // (STEP_TILES * P))
STEPS += STEPS % 2
ITERS = STEPS // 2
TILES = (STEPS + 1) * STEP_TILES
WINDOWS = 2 * (STEPS + 1)
ACC_COLS = NODES_PAD + SLOTS
PASSES = -(-NODES // SLOTS)

M_C, M_A, M_B, M_D, M_F, MSG = 0, 96, 160, 224, 320, 416
W_AB, W_C, W_F, W_D = 0, 128, 160, 192
TURNED_AT = (0, 192, 96)
HALF = 160
BANK = 512

SC_S = 1.0 / math.sqrt(64.0)
SC_V = 1.0 / math.sqrt(32.0)
LIN2 = 0.25 / math.sqrt(HID)
LIN2_S = LIN2 / math.sqrt(96.0)
LIN2_V = LIN2 / math.sqrt(128.0)


def build(nc, x, a_t, src_t, dst_t, ea_t, es_t, lin1_ws, lin1_wv, fc_w1, fc_w2, sc_ws, sc_wv,
          lin2_ws, lin2_wv, y):
    table = nc.dram_tensor("h_table", (NODES_PAD, FEAT), F32, kind="Internal").ap()
    ctx = ExitStack()
    with ctx:
        def sb(name, shape, dt=F32):
            return ctx.enter_context(nc.sbuf_tensor(name, shape, dt))

        k = dict(
            ident=sb("ident", [P, P]), iota=sb("iota", [P, SLOTS]),
            wv=sb("wv", [P, 5, OUTS]), ws=sb("ws", [P, 3, OUTS]),
            fc1=sb("fc1", [P, P]), fc2=sb("fc2", [P, WNUM]),
            l1s=sb("l1s", [NS, NS]), l1v=sb("l1v", [VEC, VEC]),
            scs=sb("scs", [NS, OUTS]), scv=sb("scv", [VEC, OUTS]),
            a=sb("a", [P, NODE_TILES]),
            src=sb("src_sb", [P, TILES], I32), ea=sb("ea", [P, TILES, 4]),
            rel=sb("rel", [P, TILES]),
            base=sb("base", [1, 2 + WINDOWS], I32), span=sb("span", [1, 1], I32),
            acc=sb("acc", [OUTS, 2, ACC_COLS]),
        )
        setup(nc, k, a_t, src_t, dst_t, ea_t, lin1_ws, lin1_wv, fc_w1, fc_w2, sc_ws, sc_wv,
              lin2_ws, lin2_wv)
        node_stage(nc, k, x, table)
        with ExitStack() as inner:
            bufs = edge_buffers(nc, inner)
            edge_pass(nc, k, bufs, table, es_t, "first")
            further_passes(nc, k, bufs, table, es_t)
        finish_stage(nc, k, x, y)


def setup(nc, k, a_t, src_t, dst_t, ea_t, lin1_ws, lin1_wv, fc_w1, fc_w2, sc_ws, sc_wv,
          lin2_ws, lin2_wv):
    chunks = [(c, min(P, WINDOWS - c)) for c in range(0, WINDOWS, P)]
    nch = len(chunks)
    with ExitStack() as ctx:
        def sb(name, shape, dt=F32):
            return ctx.enter_context(nc.sbuf_tensor(name, shape, dt))

        def sem(name):
            return ctx.enter_context(nc.semaphore(name))

        dst_i = sb("dst_i", [P, TILES], I32)
        least = sb("least", [P, WINDOWS])
        most = sb("most", [P, WINDOWS])
        ends = sb("ends", [P, 2, nch])
        width = sb("width", [P, 2])
        diag = sb("diag", [P, nch, P])
        base_all = sb("base_all", [P, WINDOWS])
        ones = sb("ones", [P, P])
        turned = [ctx.enter_context(nc.psum_tensor(f"turned{n}", [P, nch, P], F32)) for n in range(2)]
        spread = ctx.enter_context(nc.psum_tensor("spread", [P, 2 * BANK], F32))
        s_zero = sem("zeroed")
        s_ident = sem("ident_ready")
        s_w = sem("weights_in")
        s_dst = sem("dst_in")
        s_tab = sem("tables_in")
        s_ends = sem("window_ends_ready")
        s_turned = sem("ends_turned")
        s_diag = sem("diag_ready")
        s_spread = sem("bases_spread")
        s_width = sem("width_ready")
        s_wturned = sem("width_turned")
        s_chain = sem("vector_chain")
        block = ctx.enter_context(nc.Block())
        loads = []

        @block.sync
        def _(sp):
            sp.dma_start(dst_i[:, :], dst_t).then_inc(s_dst, 16)
            sp.wait_ge(s_zero, 4)
            wv, ws = k["wv"], k["ws"]
            to = [
                (k["fc1"][0:64, 0:64], fc_w1), (k["fc1"][64:128, 64:128], fc_w1),
                (k["fc2"][0:64, :], fc_w2), (k["fc2"][64:128, :], fc_w2),
                (k["l1s"][:, :], lin1_ws), (k["scs"][:, :], sc_ws),
                (ws[64:128, 0, :], lin2_ws[0:64, :]),
                (ws[32:64, 1, :], lin2_ws[64:96, :]), (ws[32:64, 2, :], lin2_ws[64:96, :]),
                (ws[64:96, 2, :], lin2_ws[64:96, :]),
            ]
            for c in range(3):
                d = slice(NV * c, NV * c + NV)
                to += [(k["l1v"][d, d], lin1_wv), (k["scv"][d, d], sc_wv)]
                to += [(wv[0:64, c, d], lin2_wv[0:64, :])]
                o1, o2 = [n for n in range(3) if n != c]
                to += [(wv[64:96, c, NV * o2:NV * o2 + NV], lin2_wv[96:128, :]),
                       (wv[96:128, c, NV * o1:NV * o1 + NV], lin2_wv[96:128, :])]
            to += [(wv[0:32, 3, 32:64], lin2_wv[64:96, :]), (wv[32:64, 3, 64:96], lin2_wv[64:96, :]),
                   (wv[64:96, 4, 0:32], lin2_wv[64:96, :])]
            for dst, of in to:
                sp.dma_start(dst, of).then_inc(s_w, 16)
            loads.append(len(to))
            sp.wait_ge(s_tab, 48)

        @block.scalar
        def _(act):
            act.dma_start(k["src"][:, :], src_t).then_inc(s_tab, 16)
            act.dma_start(k["ea"][:, :, :], ea_t).then_inc(s_tab, 16)
            act.dma_start(k["a"][:, :], a_t).then_inc(s_tab, 16)

        @block.gpsimd
        def _(pool):
            pool.memset(k["ident"][:, :], 0.0).then_inc(s_ident, 1)
            pool.wait_ge(s_ident, 1)
            pool.affine_select(out=k["ident"][:, :], in_=k["ident"][:, :], compare_op=ALU.not_equal,
                               fill=1.0, base=0, pattern=[[-1, P]], channel_multiplier=1)\
                .then_inc(s_ident, 1)
            pool.iota(k["iota"][:, :], pattern=[[1, SLOTS]], base=0, channel_multiplier=0,
                      allow_small_or_imprecise_dtypes=True).then_inc(s_ident, 1)
            pool.memset(ones[:, :], 1.0).then_inc(s_ident, 1)
            pool.memset(k["acc"][:, :, NODES_PAD:ACC_COLS], 0.0).then_inc(s_ident, 1)

        @block.vector
        def _(dve):
            for t in ("wv", "ws"):
                dve.memset(k[t][:, :, :], 0.0).then_inc(s_zero, 1)
            dve.memset(k["fc1"][:, :], 0.0).then_inc(s_zero, 1)
            dve.memset(k["l1v"][:, :], 0.0)
            dve.memset(k["scv"][:, :], 0.0).then_inc(s_zero, 1)
            dve.memset(ends[:, :, :], 0.0).then_inc(s_chain, 1)
            dve.wait_ge(s_dst, 16)
            dve.tensor_copy(k["rel"][:, :], dst_i[:, :]).then_inc(s_chain, 1)
            dve.wait_ge(s_chain, 2)
            by_window = k["rel"][:, :].rearrange("p (w t) -> p w t", t=TILES_W)
            dve.tensor_reduce(least[:, :], by_window, axis=AX.X, op=ALU.min).then_inc(s_ends, 1)
            dve.tensor_reduce(most[:, :], by_window, axis=AX.X, op=ALU.max).then_inc(s_ends, 1)
            dve.wait_ge(s_turned, 2)
            for n, op in ((0, ALU.min), (1, ALU.max)):
                for j, (_, m) in enumerate(chunks):
                    dve.tensor_reduce(ends[0:m, n, j:j + 1], turned[n][0:m, j, :], axis=AX.X, op=op)\
                       .then_inc(s_chain, 1)
            dve.wait_ge(s_chain, 2 + 2 * nch)
            dve.wait_ge(s_ident, 3)
            for j in range(nch):
                last = dve.tensor_scalar(diag[:, j, :], k["ident"][:, :], ends[:, 0, j:j + 1], None, ALU.mult)
                last.then_inc(s_diag, 1)
            dve.tensor_sub(ends[:, 1, :], ends[:, 1, :], ends[:, 0, :]).then_inc(s_chain, 1)
            dve.wait_ge(s_chain, 3 + 2 * nch)
            dve.tensor_reduce(width[:, 0:1], ends[:, 1, :], axis=AX.X, op=ALU.max).then_inc(s_width, 1)
            dve.wait_ge(s_spread, 1)
            dve.tensor_copy(base_all[:, :], spread[:, 0:WINDOWS]).then_inc(s_chain, 1)
            dve.memset(k["base"][:, 0:2], NODES_PAD)
            dve.wait_ge(s_chain, 4 + 2 * nch)
            dve.tensor_copy(k["base"][:, 2:2 + WINDOWS], base_all[0:1, :])
            dve.tensor_tensor(by_window, by_window,
                              base_all[:, :].unsqueeze(2).broadcast_to([P, WINDOWS, TILES_W]),
                              ALU.subtract)
            dve.wait_ge(s_wturned, 1)
            dve.tensor_reduce(width[0:1, 1:2], spread[0:1, 2 * BANK - P:2 * BANK], axis=AX.X, op=ALU.max)\
               .then_inc(s_chain, 1)
            dve.wait_ge(s_chain, 5 + 2 * nch)
            dve.tensor_copy(k["span"][:, :], width[0:1, 1:2])
            dve.wait_ge(s_w, 16 * loads[0])
            dve.tensor_scalar_mul(k["l1s"][:, :], k["l1s"][:, :], SC_S)
            dve.tensor_scalar_mul(k["l1v"][:, :], k["l1v"][:, :], SC_V)
            dve.tensor_scalar_mul(k["scs"][:, :], k["scs"][:, :], SC_S)
            dve.tensor_scalar_mul(k["scv"][:, :], k["scv"][:, :], SC_V)
            wv, ws = k["wv"], k["ws"]
            dve.tensor_scalar_mul(ws[:, :, :], ws[:, :, :], LIN2_S).then_inc(s_chain, 1)
            dve.tensor_scalar_mul(wv[:, :, :], wv[:, :, :], LIN2_V).then_inc(s_chain, 1)
            dve.wait_ge(s_chain, 7 + 2 * nch)
            dve.tensor_scalar_mul(ws[32:64, 1:3, :], ws[32:64, 1:3, :], 1.0 / math.sqrt(3.0))
            dve.tensor_scalar_mul(ws[64:96, 2, :], ws[64:96, 2, :], 1.0 / math.sqrt(3.0))
            half = 1.0 / math.sqrt(2.0)
            for c in range(3):
                o1, o2 = [n for n in range(3) if n != c]
                for row, d, i in ((64, o1, o2), (96, o2, o1)):
                    w = wv[row:row + 32, c, NV * i:NV * i + NV]
                    plus = (d, c) == ((i + 1) % 3, (i + 2) % 3)
                    dve.tensor_scalar_mul(w, w, half if plus else -half)

        @block.tensor
        def _(pe):
            pe.wait_ge(s_ident, 2)
            for n, ends_of in enumerate((least, most)):
                pe.wait_ge(s_ends, n + 1)
                for j, (c, m) in enumerate(chunks):
                    last = pe.transpose(turned[n][0:m, j, :], ends_of[:, c:c + m], k["ident"][:, :])
                last.then_inc(s_turned, 1)
            pe.wait_ge(s_ident, 4)
            pe.wait_ge(s_diag, nch)
            for j, (c, m) in enumerate(chunks):
                last = pe.matmul(spread[:, c:c + m], ones[:, :], diag[:, j, 0:m], start=True, stop=True)
            last.then_inc(s_spread, 1)
            pe.wait_ge(s_width, 1)
            pe.wait_ge(s_chain, 4 + 2 * nch)
            pe.transpose(spread[0:1, 2 * BANK - P:2 * BANK], width[:, 0:1], k["ident"][:, :])\
              .then_inc(s_wturned, 1)


def node_stage(nc, k, x, table):
    TURN = 2 * GROUP
    x_v = x.rearrange("(t p) f -> p t f", p=P)
    table_v = table.rearrange("(t p) f -> p t f", p=P)
    with ExitStack() as ctx:
        def sb(name, shape, dt=F32):
            return ctx.enter_context(nc.sbuf_tensor(name, shape, dt))

        def sem(name):
            return ctx.enter_context(nc.semaphore(name))

        def pb(name):
            return ctx.enter_context(nc.psum_tensor(name, [P, BANK], F32))

        xin = sb("xin", [P, TURN, FEAT])
        stats = sb("stats", [P, TURN, 6])
        mv = sb("mv", [P, TURN, 2])
        std = sb("std", [P, TURN])
        rstd = sb("rstd", [P, TURN])
        shift = sb("shift", [P, TURN])
        h = sb("h", [P, TURN, FEAT])
        hts = sb("hts", [NS, 2, P])
        htv = sb("htv", [VEC, 2, P])
        rows = sb("rows", [P, TURN, FEAT])
        ps_t = [pb(f"node_turned{n}") for n in range(2)]
        ps_r = [pb(f"node_rows{n}") for n in range(2)]
        ps_s = [pb(f"node_self{n}") for n in range(2)]
        x_in = [sem(f"x_in{g}") for g in range(2)]
        stats_ok = sem("stats_ready")
        stats_seen = sem("stats_seen")
        mv_ok = sem("mean_var_ready")
        var_ok = sem("var_ready")
        std_ok = sem("std_ready")
        rstd_ok = sem("rstd_ready")
        shift_ok = sem("shift_ready")
        h_ok = sem("h_ready")
        turned = sem("h_turned")
        ht_ok = sem("hT_ready")
        lin_ok = sem("linear1_done")
        rows_ok = sem("rows_ready")
        self_ok = sem("self_kept")
        out_done = [sem(f"rows_out{g}") for g in range(2)]
        block = ctx.enter_context(nc.Block())

        def load(sp, turn, g):
            sp.dma_start(xin[:, g * GROUP:(g + 1) * GROUP, :],
                         x_v[:, bass.ds(turn * TURN + g * GROUP, GROUP), :]).then_inc(x_in[g], 16)

        @block.sync
        def _(sp):
            for g in range(2):
                load(sp, 0, g)
            with sp.Fori(0, NODE_ITERS - 1) as i:
                for g in range(2):
                    sp.wait_ge(h_ok, i * TURN + (g + 1) * GROUP)
                    load(sp, i + 1, g)

        @block.gpsimd
        def _(pool):
            with pool.Fori(0, NODE_ITERS) as i:
                for g in range(2):
                    pool.wait_ge(rows_ok, i * TURN + (g + 1) * GROUP)
                    pool.dma_start(table_v[:, bass.ds(i * TURN + g * GROUP, GROUP), :],
                                   rows[:, g * GROUP:(g + 1) * GROUP, :]).then_inc(out_done[g], 16)
            for g in range(2):
                pool.wait_ge(out_done[g], 16 * NODE_ITERS)

        @block.vector
        def _(dve):
            with dve.Fori(0, NODE_ITERS) as i:
                for g in range(2):
                    grp = slice(g * GROUP, (g + 1) * GROUP)
                    dve.wait_ge(x_in[g], 16 * i + 16)
                    for t in range(g * GROUP, (g + 1) * GROUP):
                        dve.bn_stats(stats[:, t, :], xin[:, t, :]).then_inc(stats_ok, 1)
                    dve.wait_ge(stats_ok, i * TURN + (g + 1) * GROUP)
                    dve.sem_inc(stats_seen, 1)
                    for t in range(g * GROUP, (g + 1) * GROUP):
                        dve.bn_aggr(mv[:, t, :], stats[:, t, :]).then_inc(mv_ok, 1)
                    dve.wait_ge(mv_ok, i * TURN + (g + 1) * GROUP)
                    dve.tensor_scalar_add(std[:, grp], mv[:, grp, 1], 1e-5).then_inc(var_ok, 1)
                for g in range(2):
                    grp = slice(g * GROUP, (g + 1) * GROUP)
                    dve.wait_ge(std_ok, 2 * i + g + 1)
                    dve.reciprocal(rstd[:, grp], std[:, grp]).then_inc(rstd_ok, 1)
                    dve.wait_ge(rstd_ok, 2 * i + g + 1)
                    dve.scalar_tensor_tensor(out=shift[:, grp], in0=mv[:, grp, 0], scalar=-1.0,
                                             in1=rstd[:, grp], op0=ALU.mult, op1=ALU.mult)\
                       .then_inc(shift_ok, 1)

                def row(t):
                    dve.wait_ge(lin_ok, i * TURN + t + 1)
                    dve.tensor_scalar(rows[:, t, :], ps_r[t % 2][:, 0:FEAT],
                                      k["a"][:, bass.ds(i * TURN + t, 1)], None, ALU.mult)\
                       .then_inc(rows_ok, 1)

                for t in range(TURN):
                    dve.wait_ge(turned, i * TURN + t + 1)
                    dve.tensor_copy(hts[:, t % 2, :], ps_t[t % 2][0:NS, 0:P])
                    dve.tensor_copy(htv[:, t % 2, :], ps_t[t % 2][0:VEC, P:2 * P]).then_inc(ht_ok, 1)
                    if t:
                        row(t - 1)
                row(TURN - 1)
                dve.wait_ge(out_done[0], 16 * i + 16)
                dve.wait_ge(out_done[1], 16 * i + 16)

        @block.scalar
        def _(act):
            with act.Fori(0, NODE_ITERS) as i:
                for g in range(2):
                    grp = slice(g * GROUP, (g + 1) * GROUP)
                    act.wait_ge(var_ok, 2 * i + g + 1)
                    act.activation(std[:, grp], std[:, grp], ACT.Sqrt).then_inc(std_ok, 1)

                def keep(t):
                    act.wait_ge(lin_ok, i * TURN + t + 1)
                    act.activation(k["acc"][:, :, bass.ds((i * TURN + t) * P, P)],
                                   ps_s[t % 2][0:OUTS, 0:2 * P].rearrange("p (a n) -> p a n", a=2),
                                   ACT.Copy).then_inc(self_ok, 1)

                for t in range(TURN):
                    if t % GROUP == 0:
                        act.wait_ge(shift_ok, 2 * i + t // GROUP + 1)
                    act.activation(h[:, t, :], xin[:, t, :], ACT.Relu, bias=shift[:, t:t + 1],
                                   scale=rstd[:, t:t + 1]).then_inc(h_ok, 1)
                    if t >= 2:
                        keep(t - 2)
                keep(TURN - 2)
                keep(TURN - 1)

        @block.tensor
        def _(pe):
            with pe.Fori(0, NODE_ITERS) as i:
                def turn(t):
                    pe.wait_ge(h_ok, i * TURN + t + 1)
                    pe.transpose(ps_t[t % 2][0:VEC, P:2 * P], h[:, t, NS:FEAT], k["ident"][:, :])
                    pe.transpose(ps_t[t % 2][0:NS, 0:P], h[:, t, 0:NS], k["ident"][:, :])\
                      .then_inc(turned, 1)

                turn(0)
                for t in range(TURN):
                    if t + 1 < TURN:
                        turn(t + 1)
                    pe.wait_ge(ht_ok, i * TURN + t + 1)
                    if t >= 2:
                        pe.wait_ge(rows_ok, i * TURN + t - 1)
                        pe.wait_ge(self_ok, i * TURN + t - 1)
                    hs, hv = hts[:, t % 2, :], htv[:, t % 2, :]
                    pe.matmul(ps_r[t % 2][:, 0:NS], hs, k["l1s"][:, :], start=True, stop=True)
                    pe.matmul(ps_r[t % 2][:, NS:FEAT], hv, k["l1v"][:, :], start=True, stop=True)
                    pe.matmul(ps_s[t % 2][0:OUTS, 0:P], k["scv"][:, :], hv, start=True, stop=True)
                    pe.matmul(ps_s[t % 2][0:OUTS, P:2 * P], k["scs"][:, :], hs, start=True, stop=True)\
                      .then_inc(lin_ok, 1)
                pe.wait_ge(rows_ok, i * TURN + TURN)
                pe.wait_ge(self_ok, i * TURN + TURN)


def edge_buffers(nc, ctx):
    def sb(name, shape, dt=F32):
        return ctx.enter_context(nc.sbuf_tensor(name, shape, dt))

    def pb(name, banks=1):
        return ctx.enter_context(nc.psum_tensor(name, [P, banks * BANK], F32))

    def sem(name):
        return ctx.enter_context(nc.semaphore(name))

    return dict(
        idx=sb("idx", [P, 2, STEP_TILES], I32),
        rows=sb("gathered", [P, 2, STEP_TILES, FEAT]),
        est=sb("edge_scalars", [P, 2, PAIRS * P]),
        hid=sb("hidden", [P, 2, PAIRS * P]),
        hot=sb("onehot", [P, STEP_TILES, SLOTS]),
        s=sb("weighted_onehot", [P, 2, STEP_TILES, 4, SLOTS]),
        msg=sb("messages", [P, 2, 2, MSG]),
        sums=sb("sums", [P, 2, 2 * HALF]),
        turned=sb("sums_turned", [P, 2, 3, P]),
        zeros=sb("zeros", [P, 3 * P]),
        w_ps=pb("weights_ps", 4), sum_ps=[pb("sums_ps_a"), pb("sums_ps_b")],
        ht_ps=pb("hidden_or_turned_ps"), out_ps=pb("out_ps"),
        zeroed=sem("zeros_ready"), primed=sem("pipeline_primed"),
        est_in=[sem(f"edge_scalars_in{u}") for u in range(2)],
        idx_ok=sem("indices_ready"), gathers_begun=sem("gathers_begun"),
        rows_in=[sem(f"rows_gathered{u}") for u in range(2)],
        hid_mm=sem("hidden_product_done"), hid_ok=sem("hidden_ready"),
        w_mm=sem("weights_done"),
        hot_ok=sem("onehot_ready"), s_ok=sem("weighted_onehot_ready"),
        msg_ok=sem("messages_ready"),
        sum_mm=sem("window_summed"), sum_ok=sem("sums_copied"),
        turn_mm=sem("sums_turned_ps"), turn_ok=sem("sums_turned_copied"),
        out_mm=sem("linear2_done"), out_added=sem("window_added"),
    )


EDGE_SEMS = ("zeroed", "primed", "est_in", "idx_ok", "gathers_begun", "rows_in", "hid_mm", "hid_ok", "w_mm", "hot_ok",
             "s_ok", "msg_ok", "sum_mm", "sum_ok", "turn_mm", "turn_ok", "out_mm", "out_added")


def edge_pass(nc, k, b, table, es_t, name):
    with ExitStack() as ctx:
        block = ctx.enter_context(nc.Block(name=f"edges_{name}"))

        def load_scalars(sp, step, u):
            sp.dma_start(b["est"][:, u, :], es_t[bass.ds(step, 1), :, :].rearrange("s p e -> p (s e)"))\
              .then_inc(b["est_in"][u], 16)

        @block.sync
        def _(sp):
            for u in range(2):
                load_scalars(sp, u, u)
            with sp.Fori(0, ITERS - 1) as i:
                for u in range(2):
                    sp.wait_ge(b["hid_mm"], 2 * i + u + 1)
                    load_scalars(sp, 2 * i + 2 + u, u)
            sp.wait_ge(b["hid_mm"], STEPS - 1)
            load_scalars(sp, STEPS, 0)
            sp.wait_ge(b["est_in"][0], 16 * (ITERS + 1))

        @block.gpsimd
        def _(pool):
            pool.memset(b["zeros"][:, :], 0.0).then_inc(b["zeroed"], 1)

            def gather(step, u, nth):
                pool.tensor_copy(b["idx"][:, u, :], k["src"][:, bass.ds(step * STEP_TILES, STEP_TILES)])\
                    .then_inc(b["idx_ok"], 1)
                pool.wait_ge(b["idx_ok"], nth)
                pool.sem_inc(b["gathers_begun"], 1)
                for t in range(STEP_TILES):
                    pool.indirect_dma_start(
                        b["rows"][:, u, t, :], None, table[:, :],
                        bass.IndirectOffsetOnAxis(ap=b["idx"][:, u, t:t + 1], axis=0))\
                        .then_inc(b["rows_in"][u], 16)

            for u in range(2):
                gather(u, u, u + 1)
            with pool.Fori(0, ITERS - 1) as i:
                for u in range(2):
                    pool.wait_ge(b["msg_ok"], (2 * i + u) * PAIRS + PAIRS)
                    gather(2 * i + 2 + u, u, 2 * i + u + 3)

        @block.scalar
        def _(act):
            def hidden(u, n):
                act.wait_ge(b["hid_mm"], n)
                act.activation(b["hid"][:, u, :], b["ht_ps"][:, 0:PAIRS * P], ACT.Silu,
                               scale=1.0 / math.sqrt(64.0)).then_inc(b["hid_ok"], 1)

            def copy_sums(half, window):
                act.wait_ge(b["sum_mm"], window + 1)
                act.activation(b["sums"][:, half, :], b["sum_ps"][half][:, 0:2 * HALF], ACT.Copy)\
                   .then_inc(b["sum_ok"], 1)

            def copy_turned(half, flush):
                act.wait_ge(b["turn_mm"], flush)
                act.activation(b["turned"][:, half, :, :],
                               b["ht_ps"][:, 0:3 * P].rearrange("p (a n) -> p a n", a=3), ACT.Copy)\
                   .then_inc(b["turn_ok"], 1)

            act.wait_ge(b["zeroed"], 1)
            act.activation(b["turned"][:, 0, :, :],
                           b["zeros"][:, :].rearrange("p (a n) -> p a n", a=3), ACT.Copy)\
               .then_inc(b["primed"], 1)
            act.activation(b["sums"][:, 1, :], b["zeros"][:, 0:2 * HALF], ACT.Copy)\
               .then_inc(b["sum_ok"], 1)
            hidden(0, 1)
            with act.Fori(0, ITERS) as i:
                for u in range(2):
                    step = 2 * i + u
                    copy_turned(1, 2 * step + 1)
                    hidden(1 - u, step + 2)
                    copy_sums(0, 2 * step)
                    copy_turned(0, 2 * step + 2)
                    copy_sums(1, 2 * step + 1)
            copy_turned(1, 2 * STEPS + 1)

        @block.vector
        def _(dve):
            def onehots(step, u, nth):
                dve.tensor_tensor(
                    b["hot"][:, :, :],
                    k["iota"][:, :].unsqueeze(1).broadcast_to([P, STEP_TILES, SLOTS]),
                    k["rel"][:, bass.ds(step * STEP_TILES, STEP_TILES)].unsqueeze(2)
                    .broadcast_to([P, STEP_TILES, SLOTS]), ALU.is_equal).then_inc(b["hot_ok"], 1)
                dve.wait_ge(b["hot_ok"], nth)
                dve.tensor_tensor(
                    b["s"][:, u, :, :, :],
                    b["hot"][:, :, :].unsqueeze(2).broadcast_to([P, STEP_TILES, 4, SLOTS]),
                    k["ea"][:, bass.ds(step * STEP_TILES, STEP_TILES), :].unsqueeze(3)
                    .broadcast_to([P, STEP_TILES, 4, SLOTS]), ALU.mult).then_inc(b["s_ok"], 1)

            def messages(u, p, slot, pair):
                dve.wait_ge(b["w_mm"], pair + 1)
                m = b["msg"][:, slot, :, :]
                w = b["w_ps"][:, 2 * slot * BANK:(2 * slot + 2) * BANK].rearrange("p (t c) -> p t c", t=2)
                g = b["rows"][:, u, 2 * p:2 * p + 2, :]
                dve.tensor_tensor(
                    m[:, :, M_A:M_A + 2 * NS].rearrange("p t (k c) -> p t k c", k=2),
                    w[:, :, W_AB:W_AB + 2 * NS].rearrange("p t (k c) -> p t k c", k=2),
                    g[:, :, 0:NS].unsqueeze(2).broadcast_to([P, 2, 2, NS]), ALU.mult)
                for at, of in ((M_C, W_C), (M_D, W_D), (M_F, W_F)):
                    last = dve.tensor_tensor(
                        m[:, :, at:at + VEC].rearrange("p t (k c) -> p t k c", k=3),
                        w[:, :, of:of + NV].unsqueeze(2).broadcast_to([P, 2, 3, NV]),
                        g[:, :, NS:FEAT].rearrange("p t (k c) -> p t k c", k=3), ALU.mult)
                last.then_inc(b["msg_ok"], 1)

            def add(flush, base):
                dve.wait_ge(b["out_mm"], flush + 1)
                a = k["acc"][:, :, bass.ds(base, SLOTS)]
                dve.tensor_tensor(a, a, b["out_ps"][0:OUTS, 0:2 * SLOTS].rearrange("p (a n) -> p a n", a=2),
                                  ALU.add).then_inc(b["out_added"], 1)

            def bases(first, n):
                return nc.values_load_multi_w_load_instructions(
                    k["base"][0:1, bass.ds(first, n)], engines=(mybir.EngineType.DVE,), min_val=0,
                    max_val=NODES_PAD, skip_runtime_bounds_check_because="least dst, or the pad")[1]

            onehots(0, 0, 1)
            with dve.Fori(0, ITERS) as i:
                at = bases(4 * i, 4)
                for u in range(2):
                    step = 2 * i + u
                    dve.wait_ge(b["rows_in"][u], (i + 1) * 16 * STEP_TILES)
                    messages(u, 0, (PAIRS * u) % 2, PAIRS * step)
                    add(2 * step, at[2 * u])
                    messages(u, 1, (PAIRS * u + 1) % 2, PAIRS * step + 1)
                    dve.wait_ge(b["s_ok"], step + 1)
                    onehots(step + 1, 1 - u, step + 2)
                    messages(u, 2, (PAIRS * u + 2) % 2, PAIRS * step + 2)
                    add(2 * step + 1, at[2 * u + 1])
            at = bases(2 * STEPS, 2)
            add(2 * STEPS, at[0])
            add(2 * STEPS + 1, at[1])

        @block.tensor
        def _(pe):
            def hidden(u, nth):
                pe.wait_ge(b["est_in"][u], 16 * nth)
                pe.matmul(b["ht_ps"][:, 0:PAIRS * P], k["fc1"][:, :], b["est"][:, u, :],
                          start=True, stop=True).then_inc(b["hid_mm"], 1)

            def weights(u, p, slot):
                for t in range(2):
                    half = slice(64 * t, 64 * t + 64)
                    last = pe.matmul(b["w_ps"][:, (2 * slot + t) * BANK:(2 * slot + t) * BANK + WNUM],
                                     b["hid"][half, u, p * P:(p + 1) * P], k["fc2"][half, :],
                                     start=True, stop=True)
                last.then_inc(b["w_mm"], 1)

            def sum_tile(u, t, slot):
                first, end = t % TILES_W == 0, t % TILES_W == TILES_W - 1
                ps = b["sum_ps"][t // TILES_W]
                m = b["msg"][:, slot, t % 2, :]
                s0, sx, sy, sz = (b["s"][:, u, t, c, :] for c in range(4))
                dxz_fy = m[:, M_D:M_D + 6 * NV].rearrange("p (k c) -> p k c", c=2 * NV)[:, :, 0:NV]
                lo, hi = ps[0:64, :], ps[64:128, :]
                for out, lhs, rhs, start, stop in (
                    (lo[:, HALF:2 * HALF], s0, m[:, M_C:M_C + HALF], first, end),
                    (hi[:, HALF + NV:2 * HALF], sz, m[:, M_B:M_B + P], first, end),
                    (lo[:, 0:NS], sx, m[:, M_B:M_B + NS], False, end),
                    (hi[:, 0:NS], sy, m[:, M_B:M_B + NS], False, end),
                    (lo[:, NS:HALF], sx, m[:, M_D + NV:M_D + 4 * NV], False, end),
                    (hi[:, NS:HALF], sy, dxz_fy, False, end),
                    (hi[:, HALF:HALF + NV], sz, m[:, M_F + 2 * NV:MSG], False, end),
                ):
                    last = pe.matmul(out, lhs, rhs, start=start, stop=stop, skip_group_check=True)
                return last

            def turn(half):
                sums = b["sums"][:, half, :]
                for n, c in enumerate(TURNED_AT):
                    last = pe.transpose(b["ht_ps"][:, n * P:(n + 1) * P], sums[:, c:c + P], k["ident"][:, :])
                last.then_inc(b["turn_mm"], 1)

            def linear2(half):
                t = b["turned"][:, half, :, :]
                lo, hi = slice(0, SLOTS), slice(SLOTS, P)
                wv, ws = k["wv"], k["ws"]
                vec = [(wv[:, 0, :], t[:, 0, lo]), (wv[:, 1, :], t[:, 0, hi]), (wv[:, 3, :], t[:, 1, lo]),
                       (wv[:, 2, :], t[:, 1, hi]), (wv[:, 4, :], t[:, 2, lo])]
                sca = [(ws[:, 0, :], t[:, 1, lo]), (ws[:, 1, :], t[:, 2, lo]), (ws[:, 2, :], t[:, 2, hi])]
                for n, (w, r) in enumerate(vec):
                    pe.matmul(b["out_ps"][0:OUTS, lo], w, r, start=n == 0, stop=n == len(vec) - 1)
                for n, (w, r) in enumerate(sca):
                    last = pe.matmul(b["out_ps"][0:OUTS, hi], w, r, start=n == 0, stop=n == len(sca) - 1)
                last.then_inc(b["out_mm"], 1)

            hidden(0, 1)
            pe.wait_ge(b["primed"], 1)
            linear2(0)
            pe.wait_ge(b["hid_ok"], 1)
            weights(0, 0, 0)
            weights(0, 1, 1)
            pe.wait_ge(b["s_ok"], 1)
            with pe.Fori(0, ITERS) as i:
                for u in range(2):
                    step = 2 * i + u
                    even = (PAIRS * u) % 2
                    pe.wait_ge(b["msg_ok"], PAIRS * step + 1)
                    sum_tile(u, 0, even)
                    pe.wait_ge(b["sum_ok"], 2 * step + 1)
                    turn(1)
                    sum_tile(u, 1, even)
                    weights(u, 2, even)
                    pe.wait_ge(b["turn_ok"], 2 * step + 1)
                    hidden(1 - u, i + 1 + u)
                    pe.wait_ge(b["msg_ok"], PAIRS * step + 2)
                    sum_tile(u, 2, 1 - even).then_inc(b["sum_mm"], 1)
                    pe.wait_ge(b["out_added"], 2 * step + 1)
                    linear2(1)
                    sum_tile(u, 3, 1 - even)
                    pe.wait_ge(b["hid_ok"], step + 2)
                    weights(1 - u, 0, 1 - even)
                    pe.wait_ge(b["sum_ok"], 2 * step + 2)
                    turn(0)
                    pe.wait_ge(b["msg_ok"], PAIRS * step + 3)
                    sum_tile(u, 4, even)
                    sum_tile(u, 5, even).then_inc(b["sum_mm"], 1)
                    weights(1 - u, 1, even)
                    pe.wait_ge(b["turn_ok"], 2 * step + 2)
                    pe.wait_ge(b["out_added"], 2 * step + 2)
                    linear2(0)
            pe.wait_ge(b["sum_ok"], 2 * STEPS + 1)
            turn(1)
            pe.wait_ge(b["turn_ok"], 2 * STEPS + 1)
            pe.wait_ge(b["out_added"], 2 * STEPS + 1)
            linear2(1)


def further_passes(nc, k, b, table, es_t):
    widest = nc.values_load(k["span"][0:1, 0:1], min_val=0, max_val=NODES - 1,
                            skip_runtime_bounds_check_because="a difference of two dst")
    with nc.If(widest >= SLOTS):
        with nc.Fori(1, PASSES) as n:
            with nc.If(widest >= n * SLOTS):
                with ExitStack() as ctx:
                    block = ctx.enter_context(nc.Block(name="move_windows"))

                    @block.vector
                    def _(dve):
                        dve.tensor_scalar_add(k["rel"][:, :], k["rel"][:, :], -float(SLOTS))
                        dve.tensor_scalar(k["base"][:, :], k["base"][:, :], float(SLOTS), float(NODES_PAD),
                                          ALU.add, ALU.min)

                    @block.gpsimd
                    def _(pool):
                        for name in EDGE_SEMS:
                            sems = b[name] if isinstance(b[name], list) else [b[name]]
                            for s in sems:
                                pool.sem_clear(s)
                edge_pass(nc, k, b, table, es_t, "further")


def finish_stage(nc, k, x, y):
    TURN = 2 * GROUP
    x_v = x.rearrange("(t p) f -> p t f", p=P)
    y_v = y.rearrange("(t p) f -> p t f", p=P)
    with ExitStack() as ctx:
        def sb(name, shape, dt=F32):
            return ctx.enter_context(nc.sbuf_tensor(name, shape, dt))

        def sem(name):
            return ctx.enter_context(nc.semaphore(name))

        xin = sb("x_again", [P, TURN, FEAT])
        part = sb("acc_part", [OUTS, 2, 2, P])
        sig = sb("sigmoid", [P, 2, OUTS])
        gated = sb("gated", [P, 2, FEAT])
        out = sb("out_rows", [P, TURN, FEAT])
        ps = [ctx.enter_context(nc.psum_tensor(f"pre_ps{n}", [P, BANK], F32)) for n in range(2)]
        x_in = [sem(f"x_again_in{g}") for g in range(2)]
        part_ok = sem("part_ready")
        pre_ok = sem("pre_ready")
        sig_ok = sem("sigmoid_ready")
        gated_ok = sem("gated_ready")
        rows_ok = sem("out_rows_ready")
        out_done = [sem(f"out_done{g}") for g in range(2)]
        block = ctx.enter_context(nc.Block())

        def load(sp, turn, g):
            sp.dma_start(xin[:, g * GROUP:(g + 1) * GROUP, :],
                         x_v[:, bass.ds(turn * TURN + g * GROUP, GROUP), :]).then_inc(x_in[g], 16)

        @block.sync
        def _(sp):
            for g in range(2):
                load(sp, 0, g)
            with sp.Fori(0, NODE_ITERS - 1) as i:
                for g in range(2):
                    sp.wait_ge(rows_ok, i * TURN + (g + 1) * GROUP)
                    load(sp, i + 1, g)

        @block.gpsimd
        def _(pool):
            with pool.Fori(0, NODE_ITERS) as i:
                for g in range(2):
                    pool.wait_ge(rows_ok, i * TURN + (g + 1) * GROUP)
                    pool.dma_start(y_v[:, bass.ds(i * TURN + g * GROUP, GROUP), :],
                                   out[:, g * GROUP:(g + 1) * GROUP, :]).then_inc(out_done[g], 16)
            for g in range(2):
                pool.wait_ge(out_done[g], 16 * NODE_ITERS)

        @block.scalar
        def _(act):
            with act.Fori(0, NODE_ITERS) as i:
                def part_of(t):
                    act.activation(part[:, t % 2, :, :], k["acc"][:, :, bass.ds((i * TURN + t) * P, P)],
                                   ACT.Copy).then_inc(part_ok, 1)

                part_of(0)
                for t in range(TURN):
                    if t + 1 < TURN:
                        if t >= 1:
                            act.wait_ge(pre_ok, i * TURN + t)
                        part_of(t + 1)
                    act.wait_ge(pre_ok, i * TURN + t + 1)
                    if t >= 2:
                        act.wait_ge(gated_ok, i * TURN + t - 1)
                    act.activation(sig[:, t % 2, :], ps[t % 2][:, OUTS:2 * OUTS], ACT.Sigmoid,
                                   scale=k["a"][:, bass.ds(i * TURN + t, 1)]).then_inc(sig_ok, 1)
                act.wait_ge(gated_ok, i * TURN + TURN)

        @block.tensor
        def _(pe):
            with pe.Fori(0, NODE_ITERS) as i:
                for t in range(TURN):
                    pe.wait_ge(part_ok, i * TURN + t + 1)
                    if t >= 2:
                        pe.wait_ge(gated_ok, i * TURN + t - 1)
                    for n in range(2):
                        last = pe.transpose(ps[t % 2][:, n * OUTS:(n + 1) * OUTS], part[:, t % 2, n, :],
                                            k["ident"][0:OUTS, 0:OUTS])
                    last.then_inc(pre_ok, 1)
                pe.wait_ge(gated_ok, i * TURN + TURN)

        @block.vector
        def _(dve):
            with dve.Fori(0, NODE_ITERS) as i:
                for t in range(TURN):
                    if t % GROUP == 0:
                        dve.wait_ge(x_in[t // GROUP], 16 * i + 16)
                    a = k["a"][:, bass.ds(i * TURN + t, 1)]
                    dve.wait_ge(sig_ok, i * TURN + t + 1)
                    dve.scalar_tensor_tensor(out=gated[:, t % 2, 0:NS], in0=ps[t % 2][:, OUTS:OUTS + NS],
                                             scalar=a, in1=sig[:, t % 2, 0:NS], op0=ALU.mult, op1=ALU.mult)
                    dve.scalar_tensor_tensor(
                        out=gated[:, t % 2, NS:FEAT].rearrange("p (i c) -> p i c", i=3),
                        in0=ps[t % 2][:, 0:VEC].rearrange("p (i c) -> p i c", i=3), scalar=a,
                        in1=sig[:, t % 2, NS:OUTS].unsqueeze(1).broadcast_to([P, 3, NV]),
                        op0=ALU.mult, op1=ALU.mult).then_inc(gated_ok, 1)
                    dve.wait_ge(gated_ok, i * TURN + t + 1)
                    dve.tensor_add(out[:, t, :], gated[:, t % 2, :], xin[:, t, :]).then_inc(rows_ok, 1)
                dve.wait_ge(out_done[0], 16 * i + 16)
                dve.wait_ge(out_done[1], 16 * i + 16)


def kernel(x, src, dst, edge_attr_4, edge_attr_64, node_vec1, L0_gnn_lin1_ws, L0_gnn_lin1_wv,
           L0_gnn_fc_w1, L0_gnn_fc_w2, L0_gnn_sc_ws, L0_gnn_sc_wv, L0_gnn_lin2_ws, L0_gnn_lin2_wv):
    import numpy as np
    import concourse.bacc as bacc
    from concourse.bass_utils import run_bass_kernel_spmd

    x = np.asarray(x)
    nodes = np.zeros((NODES_PAD, FEAT), np.float32)
    nodes[:NODES, :NS] = x[:, :NS]
    nodes[:NODES, NS:] = x[:, NS:].reshape(NODES, NV, 3).transpose(0, 2, 1).reshape(NODES, VEC)
    attr = np.zeros((NODES_PAD,), np.float32)
    attr[:NODES] = np.asarray(node_vec1)[:, 0]
    more = TILES * P - EDGES
    tiled = lambda v: np.ascontiguousarray(v.reshape(TILES, P).T)
    scalars = np.zeros((STEPS + 1, PAIRS, 2, P, NS), np.float32)
    scalars.reshape(-1, NS)[:EDGES] = np.asarray(edge_attr_64)
    ea = np.pad(np.asarray(edge_attr_4), ((0, more), (0, 0)))
    arrays = dict(
        x=nodes, node_attr=np.ascontiguousarray(attr.reshape(NODE_TILES, P).T),
        src=tiled(np.pad(np.asarray(src), (0, more))),
        dst=tiled(np.pad(np.asarray(dst), (0, more), mode="edge")),
        edge_attr=np.ascontiguousarray(ea.reshape(TILES, P, 4).transpose(1, 0, 2)),
        edge_scalars=np.ascontiguousarray(scalars.transpose(0, 2, 4, 1, 3).reshape(STEPS + 1, P, PAIRS * P)),
        lin1_ws=L0_gnn_lin1_ws, lin1_wv=L0_gnn_lin1_wv, fc_w1=L0_gnn_fc_w1, fc_w2=L0_gnn_fc_w2,
        sc_ws=L0_gnn_sc_ws, sc_wv=L0_gnn_sc_wv, lin2_ws=L0_gnn_lin2_ws, lin2_wv=L0_gnn_lin2_wv)
    arrays = {f"in_{n}": np.ascontiguousarray(v) for n, v in arrays.items()}

    nc = bacc.Bacc("TRN2", target_bir_lowering=False, num_devices=1)
    args = [nc.dram_tensor(n, v.shape, mybir.dt.from_np(v.dtype), kind="ExternalInput").ap()
            for n, v in arrays.items()]
    args.append(nc.dram_tensor("y", (NODES_PAD, FEAT), F32, kind="ExternalOutput").ap())
    build(nc, *args)
    got = np.asarray(run_bass_kernel_spmd(nc, [arrays], core_ids=[0]).results[0]["y"])[:NODES]
    out = np.empty((NODES, FEAT), np.float32)
    out[:, :NS] = got[:, :NS]
    out[:, NS:] = got[:, NS:].reshape(NODES, 3, NV).transpose(0, 2, 1).reshape(NODES, VEC)
    return out
```

```python
import math
from contextlib import ExitStack

import concourse.bass as bass
from concourse import mybir

F32 = mybir.dt.float32
I32 = mybir.dt.int32
F32R = mybir.dt.float32r
ALU = mybir.AluOpType
ACT = mybir.ActivationFunctionType
AX = mybir.AxisListType

P = 128
NODES, EDGES, FEAT = 12500, 200000, 160
NS, NV, HID, WNUM = 64, 32, 64, 224
VEC = 3 * NV
OUTS = 96

NODE_TILES = -(-NODES // P)
NODES_PAD = NODE_TILES * P
GROUP = 7
NODE_ITERS = NODE_TILES // (2 * GROUP)
assert NODE_ITERS * 2 * GROUP == NODE_TILES

TILES_W = 3
SLOTS = 64
STEP_TILES = 2 * TILES_W
PAIRS = STEP_TILES // 2
STEPS = -(-EDGES // (STEP_TILES * P))
STEPS += STEPS % 2
ITERS = STEPS // 2
TILES = (STEPS + 1) * STEP_TILES
WINDOWS = 2 * (STEPS + 1)
ACC_COLS = NODES_PAD + SLOTS
PASSES = -(-NODES // SLOTS)

M_A, M_C, M_FZ, M_DX, M_DY, M_B, M_DZ, M_FX, M_FY, MSG = 0, 64, 160, 192, 224, 256, 320, 352, 384, 416
MSG_ROW = M_DX + 2 * (M_FY - M_DX)
W_AB, W_C, W_F, W_D = 0, 128, 160, 192
TURNED_AT = (0, 192, 96)
B_ROW = (32, 0, 64)
CROSS = ((0, 0, 2, -1), (0, 96, 1, 1), (1, 64, 0, -1), (1, 96, 2, 1), (2, 0, 1, -1), (2, 32, 0, 1))
HALF = 160
BANK = 512

SC_S = 1.0 / math.sqrt(64.0)
SC_V = 1.0 / math.sqrt(32.0)
LIN2 = 0.25 / math.sqrt(HID)
LIN2_S = LIN2 / math.sqrt(96.0)
LIN2_V = LIN2 / math.sqrt(128.0)


def build(nc, x, a_t, src_t, dst_t, ea_t, es_t, lin1_ws, lin1_wv, fc_w1, fc_w2, sc_ws, sc_wv,
          lin2_ws, lin2_wv, y):
    table = nc.dram_tensor("h_table", (NODES_PAD, FEAT), F32, kind="Internal").ap()
    ctx = ExitStack()
    with ctx:
        def sb(name, shape, dt=F32):
            return ctx.enter_context(nc.sbuf_tensor(name, shape, dt))

        k = dict(
            ident=sb("ident", [P, P]), iota=sb("iota", [P, SLOTS]),
            wv=sb("wv", [P, 4, OUTS]), ws=sb("ws", [P, 2, OUTS]),
            fc1=sb("fc1", [P, P]), fc2=sb("fc2", [P, 2, WNUM], F32R),
            l1s=sb("l1s", [NS, NS]), l1v=sb("l1v", [VEC, VEC]),
            scs=sb("scs", [NS, OUTS]), scv=sb("scv", [VEC, OUTS]),
            a=sb("a", [P, NODE_TILES]),
            src=sb("src_sb", [P, TILES], I32), ea=sb("ea", [P, TILES, 4]),
            rel=sb("rel", [P, TILES]),
            base=sb("base", [1, 2 + WINDOWS], I32), span=sb("span", [1, 1], I32),
            acc=sb("acc", [OUTS, 2, ACC_COLS]),
        )
        setup(nc, k, a_t, src_t, dst_t, ea_t, lin1_ws, lin1_wv, fc_w1, fc_w2, sc_ws, sc_wv,
              lin2_ws, lin2_wv)
        node_stage(nc, k, x, table)
        with ExitStack() as inner:
            bufs = edge_buffers(nc, inner)
            edge_pass(nc, k, bufs, table, es_t, "first")
            further_passes(nc, k, bufs, table, es_t)
        finish_stage(nc, k, x, y)


def setup(nc, k, a_t, src_t, dst_t, ea_t, lin1_ws, lin1_wv, fc_w1, fc_w2, sc_ws, sc_wv,
          lin2_ws, lin2_wv):
    chunks = [(c, min(P, WINDOWS - c)) for c in range(0, WINDOWS, P)]
    nch = len(chunks)
    with ExitStack() as ctx:
        def sb(name, shape, dt=F32):
            return ctx.enter_context(nc.sbuf_tensor(name, shape, dt))

        def sem(name):
            return ctx.enter_context(nc.semaphore(name))

        dst_i = sb("dst_i", [P, TILES], I32)
        least = sb("least", [P, WINDOWS])
        most = sb("most", [P, WINDOWS])
        ends = sb("ends", [P, 2, nch])
        width = sb("width", [P, 2])
        diag = sb("diag", [P, nch, P])
        base_all = sb("base_all", [P, WINDOWS])
        ones = sb("ones", [P, P])
        fc2_in = sb("fc2_in", [P, WNUM])
        turned = [ctx.enter_context(nc.psum_tensor(f"turned{n}", [P, nch, P], F32)) for n in range(2)]
        spread = ctx.enter_context(nc.psum_tensor("spread", [P, 2 * BANK], F32))
        s_zero = sem("zeroed")
        s_ident = sem("ident_ready")
        s_w = sem("weights_in")
        s_dst = sem("dst_in")
        s_tab = sem("tables_in")
        s_ends = sem("window_ends_ready")
        s_turned = sem("ends_turned")
        s_diag = sem("diag_ready")
        s_spread = sem("bases_spread")
        s_width = sem("width_ready")
        s_wturned = sem("width_turned")
        s_chain = sem("vector_chain")
        block = ctx.enter_context(nc.Block())
        loads = []

        @block.sync
        def _(sp):
            sp.dma_start(dst_i[:, :], dst_t).then_inc(s_dst, 16)
            sp.wait_ge(s_zero, 4)
            wv, ws = k["wv"], k["ws"]
            to = [
                (k["fc1"][0:64, 0:64], fc_w1), (k["fc1"][64:128, 64:128], fc_w1),
                (fc2_in[0:64, :], fc_w2), (fc2_in[64:128, :], fc_w2),
                (k["l1s"][:, :], lin1_ws), (k["scs"][:, :], sc_ws),
                (ws[64:128, 0, :], lin2_ws[0:64, :]),
                (ws[32:64, 0, :], lin2_ws[64:96, :]), (ws[32:64, 1, :], lin2_ws[64:96, :]),
                (ws[64:96, 1, :], lin2_ws[64:96, :]),
            ]
            for c in range(3):
                d = slice(NV * c, NV * c + NV)
                to += [(k["l1v"][d, d], lin1_wv), (k["scv"][d, d], sc_wv)]
                at = B_ROW[c]
                to += [(wv[at:at + 64, c, d], lin2_wv[0:64, :]),
                       (wv[NV + NV * c:2 * NV + NV * c, 3, d], lin2_wv[64:96, :])]
            to += [(wv[row:row + NV, c, NV * i:NV * i + NV], lin2_wv[96:128, :]) for c, row, i, _ in CROSS]
            for dst, of in to:
                sp.dma_start(dst, of).then_inc(s_w, 16)
            loads.append(len(to))
            sp.wait_ge(s_tab, 48)

        @block.scalar
        def _(act):
            act.dma_start(k["src"][:, :], src_t).then_inc(s_tab, 16)
            act.dma_start(k["ea"][:, :, :], ea_t).then_inc(s_tab, 16)
            act.dma_start(k["a"][:, :], a_t).then_inc(s_tab, 16)

        @block.gpsimd
        def _(pool):
            pool.memset(k["ident"][:, :], 0.0).then_inc(s_ident, 1)
            pool.wait_ge(s_ident, 1)
            pool.affine_select(out=k["ident"][:, :], in_=k["ident"][:, :], compare_op=ALU.not_equal,
                               fill=1.0, base=0, pattern=[[-1, P]], channel_multiplier=1)\
                .then_inc(s_ident, 1)
            pool.iota(k["iota"][:, :], pattern=[[1, SLOTS]], base=0, channel_multiplier=0,
                      allow_small_or_imprecise_dtypes=True).then_inc(s_ident, 1)
            pool.memset(ones[:, :], 1.0).then_inc(s_ident, 1)
            pool.memset(k["acc"][:, :, NODES_PAD:ACC_COLS], 0.0).then_inc(s_ident, 1)

        @block.vector
        def _(dve):
            for t in ("wv", "ws"):
                dve.memset(k[t][:, :, :], 0.0).then_inc(s_zero, 1)
            dve.memset(k["fc1"][:, :], 0.0).then_inc(s_zero, 1)
            dve.memset(k["l1v"][:, :], 0.0)
            dve.memset(k["scv"][:, :], 0.0).then_inc(s_zero, 1)
            dve.memset(ends[:, :, :], 0.0).then_inc(s_chain, 1)
            dve.wait_ge(s_dst, 16)
            dve.tensor_copy(k["rel"][:, :], dst_i[:, :]).then_inc(s_chain, 1)
            dve.wait_ge(s_chain, 2)
            by_window = k["rel"][:, :].rearrange("p (w t) -> p w t", t=TILES_W)
            dve.tensor_reduce(least[:, :], by_window, axis=AX.X, op=ALU.min).then_inc(s_ends, 1)
            dve.tensor_reduce(most[:, :], by_window, axis=AX.X, op=ALU.max).then_inc(s_ends, 1)
            dve.wait_ge(s_turned, 2)
            for n, op in ((0, ALU.min), (1, ALU.max)):
                for j, (_, m) in enumerate(chunks):
                    dve.tensor_reduce(ends[0:m, n, j:j + 1], turned[n][0:m, j, :], axis=AX.X, op=op)\
                       .then_inc(s_chain, 1)
            dve.wait_ge(s_chain, 2 + 2 * nch)
            dve.wait_ge(s_ident, 3)
            for j in range(nch):
                last = dve.tensor_scalar(diag[:, j, :], k["ident"][:, :], ends[:, 0, j:j + 1], None, ALU.mult)
                last.then_inc(s_diag, 1)
            dve.tensor_sub(ends[:, 1, :], ends[:, 1, :], ends[:, 0, :]).then_inc(s_chain, 1)
            dve.wait_ge(s_chain, 3 + 2 * nch)
            dve.tensor_reduce(width[:, 0:1], ends[:, 1, :], axis=AX.X, op=ALU.max).then_inc(s_width, 1)
            dve.wait_ge(s_spread, 1)
            dve.tensor_copy(base_all[:, :], spread[:, 0:WINDOWS]).then_inc(s_chain, 1)
            dve.memset(k["base"][:, 0:2], NODES_PAD)
            dve.wait_ge(s_chain, 4 + 2 * nch)
            dve.tensor_copy(k["base"][:, 2:2 + WINDOWS], base_all[0:1, :])
            dve.tensor_tensor(by_window, by_window,
                              base_all[:, :].unsqueeze(2).broadcast_to([P, WINDOWS, TILES_W]),
                              ALU.subtract)
            dve.wait_ge(s_wturned, 1)
            dve.tensor_reduce(width[0:1, 1:2], spread[0:1, 2 * BANK - P:2 * BANK], axis=AX.X, op=ALU.max)\
               .then_inc(s_chain, 1)
            dve.wait_ge(s_chain, 5 + 2 * nch)
            dve.tensor_copy(k["span"][:, :], width[0:1, 1:2])
            dve.wait_ge(s_w, 16 * loads[0])
            dve.tensor_scalar_mul(k["l1s"][:, :], k["l1s"][:, :], SC_S)
            dve.tensor_scalar_mul(k["l1v"][:, :], k["l1v"][:, :], SC_V)
            dve.tensor_scalar_mul(k["scs"][:, :], k["scs"][:, :], SC_S)
            dve.tensor_scalar_mul(k["scv"][:, :], k["scv"][:, :], SC_V)
            wv, ws = k["wv"], k["ws"]
            dve.tensor_scalar_mul(ws[:, :, :], ws[:, :, :], LIN2_S).then_inc(s_chain, 1)
            dve.tensor_scalar_mul(wv[:, :, :], wv[:, :, :], LIN2_V).then_inc(s_chain, 1)
            dve.wait_ge(s_chain, 7 + 2 * nch)
            dve.tensor_scalar_mul(ws[32:64, :, :], ws[32:64, :, :], 1.0 / math.sqrt(3.0))
            dve.tensor_scalar_mul(ws[64:96, 1, :], ws[64:96, 1, :], 1.0 / math.sqrt(3.0))
            for c, row, i, sign in CROSS:
                w = wv[row:row + NV, c, NV * i:NV * i + NV]
                dve.tensor_scalar_mul(w, w, sign / math.sqrt(2.0))
            dve.tensor_copy(k["fc2"][:, 0, :], fc2_in[:, :]).then_inc(s_chain, 1)
            dve.wait_ge(s_chain, 8 + 2 * nch)
            dve.tensor_sub(k["fc2"][:, 1, :], fc2_in[:, :], k["fc2"][:, 0, :].bitcast(F32))

        @block.tensor
        def _(pe):
            pe.wait_ge(s_ident, 2)
            for n, ends_of in enumerate((least, most)):
                pe.wait_ge(s_ends, n + 1)
                for j, (c, m) in enumerate(chunks):
                    last = pe.transpose(turned[n][0:m, j, :], ends_of[:, c:c + m], k["ident"][:, :])
                last.then_inc(s_turned, 1)
            pe.wait_ge(s_ident, 4)
            pe.wait_ge(s_diag, nch)
            for j, (c, m) in enumerate(chunks):
                last = pe.matmul(spread[:, c:c + m], ones[:, :], diag[:, j, 0:m], start=True, stop=True)
            last.then_inc(s_spread, 1)
            pe.wait_ge(s_width, 1)
            pe.wait_ge(s_chain, 4 + 2 * nch)
            pe.transpose(spread[0:1, 2 * BANK - P:2 * BANK], width[:, 0:1], k["ident"][:, :])\
              .then_inc(s_wturned, 1)


def node_stage(nc, k, x, table):
    TURN = 2 * GROUP
    x_v = x.rearrange("(t p) f -> p t f", p=P)
    table_v = table.rearrange("(t p) f -> p t f", p=P)
    with ExitStack() as ctx:
        def sb(name, shape, dt=F32):
            return ctx.enter_context(nc.sbuf_tensor(name, shape, dt))

        def sem(name):
            return ctx.enter_context(nc.semaphore(name))

        def pb(name):
            return ctx.enter_context(nc.psum_tensor(name, [P, BANK], F32))

        xin = sb("xin", [P, TURN, FEAT])
        stats = sb("stats", [P, TURN, 6])
        mv = sb("mv", [P, TURN, 2])
        std = sb("std", [P, TURN])
        rstd = sb("rstd", [P, TURN])
        shift = sb("shift", [P, TURN])
        h = sb("h", [P, TURN, FEAT])
        hts = sb("hts", [NS, 2, P])
        htv = sb("htv", [VEC, 2, P])
        rows = sb("rows", [P, TURN, FEAT])
        ps_t = [pb(f"node_turned{n}") for n in range(2)]
        ps_r = [pb(f"node_rows{n}") for n in range(2)]
        ps_s = [pb(f"node_self{n}") for n in range(2)]
        x_in = [sem(f"x_in{g}") for g in range(2)]
        stats_ok = sem("stats_ready")
        stats_seen = sem("stats_seen")
        mv_ok = sem("mean_var_ready")
        var_ok = sem("var_ready")
        std_ok = sem("std_ready")
        rstd_ok = sem("rstd_ready")
        shift_ok = sem("shift_ready")
        h_ok = sem("h_ready")
        turned = sem("h_turned")
        ht_ok = sem("hT_ready")
        lin_ok = sem("linear1_done")
        rows_ok = sem("rows_ready")
        self_ok = sem("self_kept")
        out_done = [sem(f"rows_out{g}") for g in range(2)]
        block = ctx.enter_context(nc.Block())

        def load(sp, turn, g):
            sp.dma_start(xin[:, g * GROUP:(g + 1) * GROUP, :],
                         x_v[:, bass.ds(turn * TURN + g * GROUP, GROUP), :]).then_inc(x_in[g], 16)

        @block.sync
        def _(sp):
            for g in range(2):
                load(sp, 0, g)
            with sp.Fori(0, NODE_ITERS - 1) as i:
                for g in range(2):
                    sp.wait_ge(h_ok, i * TURN + (g + 1) * GROUP)
                    load(sp, i + 1, g)

        @block.gpsimd
        def _(pool):
            with pool.Fori(0, NODE_ITERS) as i:
                for g in range(2):
                    pool.wait_ge(rows_ok, i * TURN + (g + 1) * GROUP)
                    pool.dma_start(table_v[:, bass.ds(i * TURN + g * GROUP, GROUP), :],
                                   rows[:, g * GROUP:(g + 1) * GROUP, :]).then_inc(out_done[g], 16)
            for g in range(2):
                pool.wait_ge(out_done[g], 16 * NODE_ITERS)

        @block.vector
        def _(dve):
            with dve.Fori(0, NODE_ITERS) as i:
                for g in range(2):
                    grp = slice(g * GROUP, (g + 1) * GROUP)
                    dve.wait_ge(x_in[g], 16 * i + 16)
                    for t in range(g * GROUP, (g + 1) * GROUP):
                        dve.bn_stats(stats[:, t, :], xin[:, t, :]).then_inc(stats_ok, 1)
                    dve.wait_ge(stats_ok, i * TURN + (g + 1) * GROUP)
                    dve.sem_inc(stats_seen, 1)
                    for t in range(g * GROUP, (g + 1) * GROUP):
                        dve.bn_aggr(mv[:, t, :], stats[:, t, :]).then_inc(mv_ok, 1)
                    dve.wait_ge(mv_ok, i * TURN + (g + 1) * GROUP)
                    dve.tensor_scalar_add(std[:, grp], mv[:, grp, 1], 1e-5).then_inc(var_ok, 1)
                for g in range(2):
                    grp = slice(g * GROUP, (g + 1) * GROUP)
                    dve.wait_ge(std_ok, 2 * i + g + 1)
                    dve.reciprocal(rstd[:, grp], std[:, grp]).then_inc(rstd_ok, 1)
                    dve.wait_ge(rstd_ok, 2 * i + g + 1)
                    dve.scalar_tensor_tensor(out=shift[:, grp], in0=mv[:, grp, 0], scalar=-1.0,
                                             in1=rstd[:, grp], op0=ALU.mult, op1=ALU.mult)\
                       .then_inc(shift_ok, 1)

                def row(t):
                    dve.wait_ge(lin_ok, i * TURN + t + 1)
                    dve.tensor_scalar(rows[:, t, :], ps_r[t % 2][:, 0:FEAT],
                                      k["a"][:, bass.ds(i * TURN + t, 1)], None, ALU.mult)\
                       .then_inc(rows_ok, 1)

                for t in range(TURN):
                    dve.wait_ge(turned, i * TURN + t + 1)
                    dve.tensor_copy(hts[:, t % 2, :], ps_t[t % 2][0:NS, 0:P])
                    dve.tensor_copy(htv[:, t % 2, :], ps_t[t % 2][0:VEC, P:2 * P]).then_inc(ht_ok, 1)
                    if t:
                        row(t - 1)
                row(TURN - 1)
                dve.wait_ge(out_done[0], 16 * i + 16)
                dve.wait_ge(out_done[1], 16 * i + 16)

        @block.scalar
        def _(act):
            with act.Fori(0, NODE_ITERS) as i:
                for g in range(2):
                    grp = slice(g * GROUP, (g + 1) * GROUP)
                    act.wait_ge(var_ok, 2 * i + g + 1)
                    act.activation(std[:, grp], std[:, grp], ACT.Sqrt).then_inc(std_ok, 1)

                def keep(t):
                    act.wait_ge(lin_ok, i * TURN + t + 1)
                    act.activation(k["acc"][:, :, bass.ds((i * TURN + t) * P, P)],
                                   ps_s[t % 2][0:OUTS, 0:2 * P].rearrange("p (a n) -> p a n", a=2),
                                   ACT.Copy).then_inc(self_ok, 1)

                for t in range(TURN):
                    if t % GROUP == 0:
                        act.wait_ge(shift_ok, 2 * i + t // GROUP + 1)
                    act.activation(h[:, t, :], xin[:, t, :], ACT.Relu, bias=shift[:, t:t + 1],
                                   scale=rstd[:, t:t + 1]).then_inc(h_ok, 1)
                    if t >= 2:
                        keep(t - 2)
                keep(TURN - 2)
                keep(TURN - 1)

        @block.tensor
        def _(pe):
            with pe.Fori(0, NODE_ITERS) as i:
                def turn(t):
                    pe.wait_ge(h_ok, i * TURN + t + 1)
                    pe.transpose(ps_t[t % 2][0:VEC, P:2 * P], h[:, t, NS:FEAT], k["ident"][:, :])
                    pe.transpose(ps_t[t % 2][0:NS, 0:P], h[:, t, 0:NS], k["ident"][:, :])\
                      .then_inc(turned, 1)

                turn(0)
                for t in range(TURN):
                    if t + 1 < TURN:
                        turn(t + 1)
                    pe.wait_ge(ht_ok, i * TURN + t + 1)
                    if t >= 2:
                        pe.wait_ge(rows_ok, i * TURN + t - 1)
                        pe.wait_ge(self_ok, i * TURN + t - 1)
                    hs, hv = hts[:, t % 2, :], htv[:, t % 2, :]
                    pe.matmul(ps_r[t % 2][:, 0:NS], hs, k["l1s"][:, :], start=True, stop=True)
                    pe.matmul(ps_r[t % 2][:, NS:FEAT], hv, k["l1v"][:, :], start=True, stop=True)
                    pe.matmul(ps_s[t % 2][0:OUTS, 0:P], k["scv"][:, :], hv, start=True, stop=True)
                    pe.matmul(ps_s[t % 2][0:OUTS, P:2 * P], k["scs"][:, :], hs, start=True, stop=True)\
                      .then_inc(lin_ok, 1)
                pe.wait_ge(rows_ok, i * TURN + TURN)
                pe.wait_ge(self_ok, i * TURN + TURN)


def edge_buffers(nc, ctx):
    def sb(name, shape, dt=F32):
        return ctx.enter_context(nc.sbuf_tensor(name, shape, dt))

    def pb(name, banks=1):
        return ctx.enter_context(nc.psum_tensor(name, [P, banks * BANK], F32))

    def sem(name):
        return ctx.enter_context(nc.semaphore(name))

    return dict(
        idx=sb("idx", [P, 2, STEP_TILES], I32),
        rows=sb("gathered", [P, 2, STEP_TILES, FEAT]),
        est=sb("edge_scalars", [P, 2, PAIRS * P]),
        hid=sb("hidden", [P, 2, PAIRS * P]),
        hid2=sb("hidden_parts", [P, 2, 2, PAIRS * P], F32R),
        hot=sb("onehot", [P, STEP_TILES, SLOTS]),
        s=sb("weighted_onehot", [P, 2, STEP_TILES, 4, SLOTS]),
        msg=sb("messages", [P, PAIRS, 2, MSG_ROW]),
        sums=sb("sums", [P, 2, 2 * HALF]),
        turned=sb("sums_turned", [P, 2, 3, P]),
        zeros=sb("zeros", [P, 3 * P]),
        w_ps=[pb(f"weights_ps{p}") for p in range(PAIRS)], sum_ps=[pb("sums_ps_a"), pb("sums_ps_b")],
        hid_ps=pb("hidden_ps"), turn_ps=pb("turned_ps"), out_ps=pb("out_ps"),
        zeroed=sem("zeros_ready"), 
        est_in=[sem(f"edge_scalars_in{u}") for u in range(2)],
        idx_ok=sem("indices_ready"), gathers_begun=sem("gathers_begun"),
        rows_in=[sem(f"rows_gathered{u}") for u in range(2)],
        hid_mm=sem("hidden_product_done"), hid_ok=sem("hidden_ready"),
        split_ok=sem("hidden_split"),
        w_mm=sem("weights_done"),
        hot_ok=sem("onehot_ready"), s_ok=sem("weighted_onehot_ready"), s_act_ok=sem("weighted_onehot_scalar_ready"),
        msg_ok=sem("messages_ready"),
        sum_mm=sem("window_summed"), sum_ok=sem("sums_copied"),
        turn_mm=sem("sums_turned_ps"), turn_ok=sem("sums_turned_copied"),
        out_mm=sem("linear2_done"), out_added=sem("window_added"),
    )


EDGE_SEMS = ("zeroed", "est_in", "idx_ok", "gathers_begun", "rows_in", "hid_mm", "hid_ok",
             "split_ok", "w_mm", "hot_ok", "s_ok", "s_act_ok", "msg_ok", "sum_mm", "sum_ok", "turn_mm", "turn_ok", "out_mm", "out_added")


def edge_pass(nc, k, b, table, es_t, name):
    with ExitStack() as ctx:
        block = ctx.enter_context(nc.Block(name=f"edges_{name}"))

        def load_scalars(sp, step, u):
            sp.dma_start(b["est"][:, u, :], es_t[bass.ds(step, 1), :, :].rearrange("s p e -> p (s e)"))\
              .then_inc(b["est_in"][u], 16)

        @block.sync
        def _(sp):
            for u in range(2):
                load_scalars(sp, u, u)
            with sp.Fori(0, ITERS - 1) as i:
                for u in range(2):
                    sp.wait_ge(b["hid_mm"], 2 * i + u + 1)
                    load_scalars(sp, 2 * i + 2 + u, u)
            sp.wait_ge(b["hid_mm"], STEPS - 1)
            load_scalars(sp, STEPS, 0)
            sp.wait_ge(b["est_in"][0], 16 * (ITERS + 1))

        @block.gpsimd
        def _(pool):
            pool.memset(b["zeros"][:, :], 0.0).then_inc(b["zeroed"], 1)

            def gather(step, u, nth):
                pool.tensor_copy(b["idx"][:, u, :], k["src"][:, bass.ds(step * STEP_TILES, STEP_TILES)])\
                    .then_inc(b["idx_ok"], 1)
                pool.wait_ge(b["idx_ok"], nth)
                pool.sem_inc(b["gathers_begun"], 1)
                for t in range(STEP_TILES):
                    pool.indirect_dma_start(
                        b["rows"][:, u, t, :], None, table[:, :],
                        bass.IndirectOffsetOnAxis(ap=b["idx"][:, u, t:t + 1], axis=0))\
                        .then_inc(b["rows_in"][u], 16)

            for u in range(2):
                gather(u, u, u + 1)
            with pool.Fori(0, ITERS - 1) as i:
                for u in range(2):
                    pool.wait_ge(b["msg_ok"], (2 * i + u) * PAIRS + PAIRS)
                    gather(2 * i + 2 + u, u, 2 * i + u + 3)
            for u in range(2):
                pool.wait_ge(b["rows_in"][u], ITERS * 16 * STEP_TILES)

        @block.scalar
        def _(act):
            def hidden(u, n):
                act.wait_ge(b["hid_mm"], n)
                scale = 1.0 / math.sqrt(64.0)
                ps = b["hid_ps"][:, 0:PAIRS * P]
                act.activation(b["hid2"][0:64, u, 0, :], ps[0:64, :], ACT.Silu, scale=scale)
                act.activation(b["hid2"][64:128, u, 1, :], ps[64:128, :], ACT.Silu, scale=scale)
                act.activation(b["hid"][:, u, :], ps, ACT.Silu, scale=scale).then_inc(b["hid_ok"], 1)

            def copy_sums(half, window):
                act.wait_ge(b["sum_mm"], window + 1)
                act.activation(b["sums"][:, half, :], b["sum_ps"][half][:, 0:2 * HALF], ACT.Copy)\
                   .then_inc(b["sum_ok"], 1)

            def copy_turned(half, flush):
                act.wait_ge(b["turn_mm"], flush)
                act.activation(b["turned"][:, half, :, :],
                               b["turn_ps"][:, 0:3 * P].rearrange("p (a n) -> p a n", a=3), ACT.Copy)\
                   .then_inc(b["turn_ok"], 1)

            def weigh(step, u):
                act.wait_ge(b["hot_ok"], step + 1)
                for t in range(STEP_TILES - 2, STEP_TILES):
                    for c in range(4):
                        last = act.activation(
                            b["s"][:, u, t, c, :], b["hot"][:, t, :], ACT.Copy,
                            scale=k["ea"][:, bass.ds(step * STEP_TILES + t, 1), c])
                last.then_inc(b["s_act_ok"], 1)

            act.wait_ge(b["zeroed"], 1)
            act.activation(b["turned"][:, 0, :, :],
                           b["zeros"][:, :].rearrange("p (a n) -> p a n", a=3), ACT.Copy)\
               .then_inc(b["turn_ok"], 1)
            act.activation(b["sums"][:, 1, :], b["zeros"][:, 0:2 * HALF], ACT.Copy)\
               .then_inc(b["sum_ok"], 1)
            hidden(0, 1)
            weigh(0, 0)
            with act.Fori(0, ITERS) as i:
                for u in range(2):
                    step = 2 * i + u
                    hidden(1 - u, step + 2)
                    copy_turned(1, 2 * step + 1)
                    copy_sums(0, 2 * step)
                    weigh(step + 1, 1 - u)
                    copy_turned(0, 2 * step + 2)
                    copy_sums(1, 2 * step + 1)
            copy_turned(1, 2 * STEPS + 1)

        @block.vector
        def _(dve):
            def onehots(step):
                dve.tensor_tensor(
                    b["hot"][:, :, :],
                    k["iota"][:, :].unsqueeze(1).broadcast_to([P, STEP_TILES, SLOTS]),
                    k["rel"][:, bass.ds(step * STEP_TILES, STEP_TILES)].unsqueeze(2)
                    .broadcast_to([P, STEP_TILES, SLOTS]), ALU.is_equal).then_inc(b["hot_ok"], 1)

            def weigh(step, u, p):
                dve.wait_ge(b["hot_ok"], step + 1)
                dve.tensor_tensor(
                    b["s"][:, u, 2 * p:2 * p + 2, :, :],
                    b["hot"][:, 2 * p:2 * p + 2, :].unsqueeze(2).broadcast_to([P, 2, 4, SLOTS]),
                    k["ea"][:, bass.ds(step * STEP_TILES + 2 * p, 2), :].unsqueeze(3)
                    .broadcast_to([P, 2, 4, SLOTS]), ALU.mult).then_inc(b["s_ok"], 1)

            def messages(u, p, pair):
                dve.wait_ge(b["w_mm"], pair + 1)
                m = b["msg"][:, p, :, :]
                w = b["w_ps"][p][:, 0:2 * WNUM].rearrange("p (t c) -> p t c", t=2)
                g = b["rows"][:, u, 2 * p:2 * p + 2, :]

                def blocks(v, at, count, stride, width):
                    near = v[:, :, at // stride * stride:at // stride * stride + count * stride]
                    off = at % stride
                    return near.rearrange("p t (k c) -> p t k c", k=count)[:, :, :, off:off + width]

                dve.tensor_tensor(
                    blocks(m, M_A, 2, M_B - M_A, NS), blocks(w, W_AB, 2, NS, NS),
                    g[:, :, 0:NS].unsqueeze(2).broadcast_to([P, 2, 2, NS]), ALU.mult)
                for at, of, n in ((M_C, W_C, 3), (M_DX, W_D, 2), (M_FX, W_F, 2)):
                    dve.tensor_tensor(
                        blocks(m, at, n, NV, NV), w[:, :, of:of + NV].unsqueeze(2).broadcast_to([P, 2, n, NV]),
                        blocks(g, NS, n, NV, NV), ALU.mult)
                dve.tensor_tensor(
                    blocks(m, M_FZ, 2, M_DZ - M_FZ, NV), blocks(w, W_F, 2, NV, NV),
                    g[:, :, NS + 2 * NV:FEAT].unsqueeze(2).broadcast_to([P, 2, 2, NV]), ALU.mult)\
                   .then_inc(b["msg_ok"], 1)

            def split(u, nth):
                dve.wait_ge(b["hid_ok"], nth)
                for t, first, second in ((0, slice(0, 64), slice(64, 128)), (1, slice(64, 128), slice(0, 64))):
                    last = dve.tensor_sub(b["hid2"][second, u, t, :], b["hid"][first, u, :],
                                          b["hid2"][first, u, t, :].bitcast(F32))
                last.then_inc(b["split_ok"], 1)

            def add(half, base):
                a = k["acc"][:, :, bass.ds(base, SLOTS)]
                out = b["out_ps"][0:OUTS, 0:2 * P].rearrange("p (a n) -> p a n", a=2)
                dve.tensor_tensor(a, a, out[:, :, half * SLOTS:(half + 1) * SLOTS], ALU.add)\
                   .then_inc(b["out_added"], 1)

            def bases(first, n):
                return nc.values_load_multi_w_load_instructions(
                    k["base"][0:1, bass.ds(first, n)], engines=(mybir.EngineType.DVE,), min_val=0,
                    max_val=NODES_PAD, skip_runtime_bounds_check_because="least dst, or the pad")[1]

            onehots(0)
            for p in range(PAIRS - 1):
                weigh(0, 0, p)
            split(0, 1)
            with dve.Fori(0, ITERS) as i:
                for u in range(2):
                    step = 2 * i + u
                    pair = PAIRS * step
                    dve.wait_ge(b["rows_in"][u], (i + 1) * 16 * STEP_TILES)
                    messages(u, 0, pair)
                    if u == 0:
                        at = bases(4 * i, 4)
                    dve.wait_ge(b["s_ok"], (PAIRS - 1) * (step + 1))
                    dve.wait_ge(b["s_act_ok"], step + 1)
                    onehots(step + 1)
                    messages(u, 1, pair + 1)
                    weigh(step + 1, 1 - u, 0)
                    split(1 - u, step + 2)
                    messages(u, 2, pair + 2)
                    dve.wait_ge(b["out_mm"], step + 1)
                    add(0, at[2 * u])
                    weigh(step + 1, 1 - u, 1)
                    dve.wait_ge(b["out_added"], 2 * step + 1)
                    add(1, at[2 * u + 1])
            at = bases(2 * STEPS, 2)
            dve.wait_ge(b["out_mm"], STEPS + 1)
            add(0, at[0])
            dve.wait_ge(b["out_added"], 2 * STEPS + 1)
            add(1, at[1])

        @block.tensor
        def _(pe):
            def hidden(u, nth):
                pe.wait_ge(b["est_in"][u], 16 * nth)
                pe.matmul(b["hid_ps"][:, 0:PAIRS * P], k["fc1"][:, :], b["est"][:, u, :],
                          start=True, stop=True).then_inc(b["hid_mm"], 1)

            def weights(u, p):
                for t in range(2):
                    for part in range(2):
                        last = pe.matmul(b["w_ps"][p][:, t * WNUM:(t + 1) * WNUM],
                                         b["hid2"][:, u, t, p * P:(p + 1) * P], k["fc2"][:, part, :],
                                         start=part == 0, stop=part == 1)
                last.then_inc(b["w_mm"], 1)

            def sum_tile(u, t):
                first, end = t % TILES_W == 0, t % TILES_W == TILES_W - 1
                ps = b["sum_ps"][t // TILES_W]
                m = b["msg"][:, t // 2, t % 2, :]
                s0, sx, sy, sz = (b["s"][:, u, t, c, :] for c in range(4))
                dx_fy = m[:, M_DX:].rearrange("p (k c) -> p k c", k=2)[:, :, 0:NV]
                lo, hi = ps[0:64, :], ps[64:128, :]
                for out, lhs, rhs, start, stop in (
                    (lo[:, HALF:2 * HALF], s0, m[:, M_A:M_A + HALF], first, end),
                    (hi[:, HALF:2 * HALF], sz, m[:, M_FZ:M_FZ + HALF], first, end),
                    (lo[:, 0:HALF], sx, m[:, M_DY:M_DY + HALF], False, end),
                    (hi[:, 0:3 * NV], sy, m[:, M_B:M_B + 3 * NV], False, end),
                    (hi[:, 3 * NV:HALF], sy, dx_fy, False, end),
                ):
                    last = pe.matmul(out, lhs, rhs, start=start, stop=stop, skip_group_check=True)
                return last

            def turn(half):
                sums = b["sums"][:, half, :]
                for n, c in enumerate(TURNED_AT):
                    last = pe.transpose(b["turn_ps"][:, n * P:(n + 1) * P], sums[:, c:c + P], k["ident"][:, :])
                last.then_inc(b["turn_mm"], 1)

            def linear2():
                def piece(n, half):
                    return b["turned"][:, :, n, half * SLOTS:(half + 1) * SLOTS]

                out = b["out_ps"][0:OUTS, :]
                wv, ws = k["wv"], k["ws"]
                vec = [(wv[:, 0, :], piece(0, 0)), (wv[:, 1, :], piece(0, 1)),
                       (wv[:, 3, :], piece(1, 0)), (wv[:, 2, :], piece(1, 1))]
                sca = [(ws[:, 0, :], piece(2, 0)), (ws[:, 1, :], piece(2, 1))]
                for n, (w, r) in enumerate(vec):
                    pe.matmul(out[:, 0:P], w, r, start=n == 0, stop=n == len(vec) - 1)
                for n, (w, r) in enumerate(sca):
                    last = pe.matmul(out[:, P:2 * P], w, r, start=n == 0, stop=n == len(sca) - 1)
                last.then_inc(b["out_mm"], 1)

            hidden(0, 1)
            pe.wait_ge(b["split_ok"], 1)
            weights(0, 0)
            weights(0, 1)
            with pe.Fori(0, ITERS) as i:
                for u in range(2):
                    step = 2 * i + u
                    pe.wait_ge(b["msg_ok"], PAIRS * step + 1)
                    hidden(1 - u, i + 1 + u)
                    sum_tile(u, 0)
                    pe.wait_ge(b["turn_ok"], 2 * step + 1)
                    pe.wait_ge(b["sum_ok"], 2 * step + 1)
                    turn(1)
                    sum_tile(u, 1)
                    weights(u, 2)
                    pe.wait_ge(b["msg_ok"], PAIRS * step + 2)
                    sum_tile(u, 2).then_inc(b["sum_mm"], 1)
                    pe.wait_ge(b["turn_ok"], 2 * step + 2)
                    linear2()
                    sum_tile(u, 3)
                    pe.wait_ge(b["split_ok"], step + 2)
                    weights(1 - u, 0)
                    pe.wait_ge(b["msg_ok"], PAIRS * step + 3)
                    pe.wait_ge(b["s_act_ok"], step + 1)
                    sum_tile(u, 4)
                    pe.wait_ge(b["sum_ok"], 2 * step + 2)
                    turn(0)
                    sum_tile(u, 5).then_inc(b["sum_mm"], 1)
                    weights(1 - u, 1)
            pe.wait_ge(b["turn_ok"], 2 * STEPS + 1)
            pe.wait_ge(b["sum_ok"], 2 * STEPS + 1)
            turn(1)
            pe.wait_ge(b["turn_ok"], 2 * STEPS + 2)
            pe.wait_ge(b["out_added"], 2 * STEPS)
            linear2()


def further_passes(nc, k, b, table, es_t):
    def widest():
        return nc.values_load(k["span"][0:1, 0:1], min_val=0, max_val=NODES - 1,
                              skip_runtime_bounds_check_because="a difference of two dst")

    with nc.If(widest() >= SLOTS):
        with nc.Fori(1, PASSES):
            with nc.If(widest() >= SLOTS):
                nc.all_engine_barrier()
                with ExitStack() as ctx:
                    block = ctx.enter_context(nc.Block(name="move_windows"))

                    @block.vector
                    def _(dve):
                        dve.tensor_scalar_add(k["rel"][:, :], k["rel"][:, :], -float(SLOTS))
                        dve.tensor_scalar_add(k["span"][:, :], k["span"][:, :], -float(SLOTS))
                        dve.tensor_scalar(k["base"][:, :], k["base"][:, :], float(SLOTS), float(NODES_PAD),
                                          ALU.add, ALU.min)

                    @block.gpsimd
                    def _(pool):
                        for s in b["rows_in"]:
                            pool.dma_reset(range(s.num, s.num + 1))
                        for name in EDGE_SEMS:
                            sems = b[name] if isinstance(b[name], list) else [b[name]]
                            for s in sems:
                                pool.sem_clear(s)
                edge_pass(nc, k, b, table, es_t, "further")


def finish_stage(nc, k, x, y):
    TURN = 2 * GROUP
    x_v = x.rearrange("(t p) f -> p t f", p=P)
    y_v = y.rearrange("(t p) f -> p t f", p=P)
    with ExitStack() as ctx:
        def sb(name, shape, dt=F32):
            return ctx.enter_context(nc.sbuf_tensor(name, shape, dt))

        def sem(name):
            return ctx.enter_context(nc.semaphore(name))

        xin = sb("x_again", [P, TURN, FEAT])
        part = sb("acc_part", [OUTS, 2, 2, P])
        sig = sb("sigmoid", [P, 2, OUTS])
        gated = sb("gated", [P, 2, FEAT])
        out = sb("out_rows", [P, TURN, FEAT])
        ps = [ctx.enter_context(nc.psum_tensor(f"pre_ps{n}", [P, BANK], F32)) for n in range(2)]
        x_in = [sem(f"x_again_in{g}") for g in range(2)]
        part_ok = sem("part_ready")
        pre_ok = sem("pre_ready")
        sig_ok = sem("sigmoid_ready")
        gated_ok = sem("gated_ready")
        rows_ok = sem("out_rows_ready")
        out_done = [sem(f"out_done{g}") for g in range(2)]
        block = ctx.enter_context(nc.Block())

        def load(sp, turn, g):
            sp.dma_start(xin[:, g * GROUP:(g + 1) * GROUP, :],
                         x_v[:, bass.ds(turn * TURN + g * GROUP, GROUP), :]).then_inc(x_in[g], 16)

        @block.sync
        def _(sp):
            for g in range(2):
                load(sp, 0, g)
            with sp.Fori(0, NODE_ITERS - 1) as i:
                for g in range(2):
                    sp.wait_ge(rows_ok, i * TURN + (g + 1) * GROUP)
                    load(sp, i + 1, g)

        @block.gpsimd
        def _(pool):
            with pool.Fori(0, NODE_ITERS) as i:
                for g in range(2):
                    pool.wait_ge(rows_ok, i * TURN + (g + 1) * GROUP)
                    pool.dma_start(y_v[:, bass.ds(i * TURN + g * GROUP, GROUP), :],
                                   out[:, g * GROUP:(g + 1) * GROUP, :]).then_inc(out_done[g], 16)
            for g in range(2):
                pool.wait_ge(out_done[g], 16 * NODE_ITERS)

        @block.scalar
        def _(act):
            with act.Fori(0, NODE_ITERS) as i:
                def part_of(t):
                    act.activation(part[:, t % 2, :, :], k["acc"][:, :, bass.ds((i * TURN + t) * P, P)],
                                   ACT.Copy).then_inc(part_ok, 1)

                part_of(0)
                for t in range(TURN):
                    if t + 1 < TURN:
                        if t >= 1:
                            act.wait_ge(pre_ok, i * TURN + t)
                        part_of(t + 1)
                    act.wait_ge(pre_ok, i * TURN + t + 1)
                    if t >= 2:
                        act.wait_ge(gated_ok, i * TURN + t - 1)
                    act.activation(sig[:, t % 2, :], ps[t % 2][:, OUTS:2 * OUTS], ACT.Sigmoid,
                                   scale=k["a"][:, bass.ds(i * TURN + t, 1)]).then_inc(sig_ok, 1)
                act.wait_ge(gated_ok, i * TURN + TURN)

        @block.tensor
        def _(pe):
            with pe.Fori(0, NODE_ITERS) as i:
                for t in range(TURN):
                    pe.wait_ge(part_ok, i * TURN + t + 1)
                    if t >= 2:
                        pe.wait_ge(gated_ok, i * TURN + t - 1)
                    for n in range(2):
                        last = pe.transpose(ps[t % 2][:, n * OUTS:(n + 1) * OUTS], part[:, t % 2, n, :],
                                            k["ident"][0:OUTS, 0:OUTS])
                    last.then_inc(pre_ok, 1)
                pe.wait_ge(gated_ok, i * TURN + TURN)

        @block.vector
        def _(dve):
            with dve.Fori(0, NODE_ITERS) as i:
                for t in range(TURN):
                    if t % GROUP == 0:
                        dve.wait_ge(x_in[t // GROUP], 16 * i + 16)
                    a = k["a"][:, bass.ds(i * TURN + t, 1)]
                    dve.wait_ge(sig_ok, i * TURN + t + 1)
                    dve.scalar_tensor_tensor(out=gated[:, t % 2, 0:NS], in0=ps[t % 2][:, OUTS:OUTS + NS],
                                             scalar=a, in1=sig[:, t % 2, 0:NS], op0=ALU.mult, op1=ALU.mult)
                    dve.scalar_tensor_tensor(
                        out=gated[:, t % 2, NS:FEAT].rearrange("p (i c) -> p i c", i=3),
                        in0=ps[t % 2][:, 0:VEC].rearrange("p (i c) -> p i c", i=3), scalar=a,
                        in1=sig[:, t % 2, NS:OUTS].unsqueeze(1).broadcast_to([P, 3, NV]),
                        op0=ALU.mult, op1=ALU.mult).then_inc(gated_ok, 1)
                    dve.wait_ge(gated_ok, i * TURN + t + 1)
                    dve.tensor_add(out[:, t, :], gated[:, t % 2, :], xin[:, t, :]).then_inc(rows_ok, 1)
                dve.wait_ge(out_done[0], 16 * i + 16)
                dve.wait_ge(out_done[1], 16 * i + 16)


def kernel(x, src, dst, edge_attr_4, edge_attr_64, node_vec1, L0_gnn_lin1_ws, L0_gnn_lin1_wv,
           L0_gnn_fc_w1, L0_gnn_fc_w2, L0_gnn_sc_ws, L0_gnn_sc_wv, L0_gnn_lin2_ws, L0_gnn_lin2_wv):
    import numpy as np
    import concourse.bacc as bacc
    from concourse.bass_utils import run_bass_kernel_spmd

    x = np.asarray(x)
    nodes = np.zeros((NODES_PAD, FEAT), np.float32)
    nodes[:NODES, :NS] = x[:, :NS]
    nodes[:NODES, NS:] = x[:, NS:].reshape(NODES, NV, 3).transpose(0, 2, 1).reshape(NODES, VEC)
    attr = np.zeros((NODES_PAD,), np.float32)
    attr[:NODES] = np.asarray(node_vec1)[:, 0]
    more = TILES * P - EDGES
    tiled = lambda v: np.ascontiguousarray(v.reshape(TILES, P).T)
    scalars = np.zeros((STEPS + 1, PAIRS, 2, P, NS), np.float32)
    scalars.reshape(-1, NS)[:EDGES] = np.asarray(edge_attr_64)
    ea = np.pad(np.asarray(edge_attr_4), ((0, more), (0, 0)))
    arrays = dict(
        x=nodes, node_attr=np.ascontiguousarray(attr.reshape(NODE_TILES, P).T),
        src=tiled(np.pad(np.asarray(src), (0, more))),
        dst=tiled(np.pad(np.asarray(dst), (0, more), mode="edge")),
        edge_attr=np.ascontiguousarray(ea.reshape(TILES, P, 4).transpose(1, 0, 2)),
        edge_scalars=np.ascontiguousarray(scalars.transpose(0, 2, 4, 1, 3).reshape(STEPS + 1, P, PAIRS * P)),
        lin1_ws=L0_gnn_lin1_ws, lin1_wv=L0_gnn_lin1_wv, fc_w1=L0_gnn_fc_w1, fc_w2=L0_gnn_fc_w2,
        sc_ws=L0_gnn_sc_ws, sc_wv=L0_gnn_sc_wv, lin2_ws=L0_gnn_lin2_ws, lin2_wv=L0_gnn_lin2_wv)
    arrays = {f"in_{n}": np.ascontiguousarray(v) for n, v in arrays.items()}

    nc = bacc.Bacc("TRN2", target_bir_lowering=False, num_devices=1)
    args = [nc.dram_tensor(n, v.shape, mybir.dt.from_np(v.dtype), kind="ExternalInput").ap()
            for n, v in arrays.items()]
    args.append(nc.dram_tensor("y", (NODES_PAD, FEAT), F32, kind="ExternalOutput").ap())
    build(nc, *args)
    got = np.asarray(run_bass_kernel_spmd(nc, [arrays], core_ids=[0]).results[0]["y"])[:NODES]
    out = np.empty((NODES, FEAT), np.float32)
    out[:, :NS] = got[:, :NS]
    out[:, NS:] = got[:, NS:].reshape(NODES, 3, NV).transpose(0, 2, 1).reshape(NODES, VEC)
    return out
```

```python
import math
from contextlib import ExitStack

import concourse.bass as bass
from concourse import mybir

F32 = mybir.dt.float32
I32 = mybir.dt.int32
F32R = mybir.dt.float32r
ALU = mybir.AluOpType
ACT = mybir.ActivationFunctionType
AX = mybir.AxisListType

P = 128
NODES, EDGES, FEAT = 12500, 200000, 160
NS, NV, HID, WNUM = 64, 32, 64, 224
VEC = 3 * NV
OUTS = 96

NODE_TILES = -(-NODES // P)
NODES_PAD = NODE_TILES * P
GROUP = 7
NODE_ITERS = NODE_TILES // (2 * GROUP)
assert NODE_ITERS * 2 * GROUP == NODE_TILES

LOADS = ((0, 4), (4, 7), (7, 11), (11, 14))

TILES_W = 3
SLOTS = 64
STEP_TILES = 2 * TILES_W
PAIRS = STEP_TILES // 2
STEPS = -(-EDGES // (STEP_TILES * P))
STEPS += STEPS % 2
ITERS = STEPS // 2
TILES = (STEPS + 1) * STEP_TILES
WINDOWS = 2 * (STEPS + 1)
ACC_COLS = NODES_PAD + SLOTS
PASSES = -(-NODES // SLOTS)

M_C, M_A, M_FY, M_FZ, M_DX, M_DY, M_B, M_DZ, M_FX, MSG = 0, 96, 160, 192, 224, 256, 288, 352, 384, 416
W_AB, W_C, W_F, W_D = 0, 128, 160, 192
SUM_X, SUM_GAP, SUM_Z, SUM_0, SUM_Y, SUMS = 0, 160, 192, 0, 160, 352
TURNED_AT = (0, 224, 96)
B_ROW = (32, 32, 64)
CROSS = ((0, 0, 2, -1), (0, 96, 1, 1), (1, 96, 0, -1), (1, 0, 2, 1), (2, 0, 1, -1), (2, 32, 0, 1))
BANK = 512

WARM_UP = 5

SC_S = 1.0 / math.sqrt(64.0)
SC_V = 1.0 / math.sqrt(32.0)
LIN2 = 0.25 / math.sqrt(HID)
LIN2_S = LIN2 / math.sqrt(96.0)
LIN2_V = LIN2 / math.sqrt(128.0)


def build(nc, x, a_t, src_t, dst_t, ea_t, es_t, lin1_ws, lin1_wv, fc_w1, fc_w2, sc_ws, sc_wv,
          lin2_ws, lin2_wv, y):
    table = nc.dram_tensor("h_table", (NODES_PAD, FEAT), F32, kind="Internal").ap()
    ctx = ExitStack()
    with ctx:
        def sb(name, shape, dt=F32):
            return ctx.enter_context(nc.sbuf_tensor(name, shape, dt))

        k = dict(
            ident=sb("ident", [P, P]), iota=sb("iota", [P, SLOTS]),
            wv=sb("wv", [P, 4, OUTS]), ws=sb("ws", [P, 2, OUTS]),
            fc1=sb("fc1", [P, P]), fc2=sb("fc2", [P, 2, WNUM], F32R),
            l1s=sb("l1s", [NS, NS]), l1v=sb("l1v", [VEC, VEC]),
            scs=sb("scs", [NS, OUTS]), scv=sb("scv", [VEC, OUTS]),
            a=sb("a", [P, NODE_TILES]),
            src=sb("src_sb", [P, TILES], I32), ea=sb("ea", [P, TILES, 4]),
            rel=sb("rel", [P, TILES]),
            base=sb("base", [1, 2 + WINDOWS], I32), span=sb("span", [1, 1], I32),
            acc=sb("acc", [OUTS, 2, ACC_COLS]),
        )
        setup(nc, k, a_t, src_t, dst_t, ea_t, lin1_ws, lin1_wv, fc_w1, fc_w2, sc_ws, sc_wv,
              lin2_ws, lin2_wv)
        node_stage(nc, k, x, table)
        with ExitStack() as inner:
            bufs = edge_buffers(nc, inner)
            edge_pass(nc, k, bufs, table, es_t, "first")
            further_passes(nc, k, bufs, table, es_t)
        finish_stage(nc, k, x, y)


def setup(nc, k, a_t, src_t, dst_t, ea_t, lin1_ws, lin1_wv, fc_w1, fc_w2, sc_ws, sc_wv,
          lin2_ws, lin2_wv):
    chunks = [(c, min(P, WINDOWS - c)) for c in range(0, WINDOWS, P)]
    nch = len(chunks)
    with ExitStack() as ctx:
        def sb(name, shape, dt=F32):
            return ctx.enter_context(nc.sbuf_tensor(name, shape, dt))

        def sem(name):
            return ctx.enter_context(nc.semaphore(name))

        dst_i = sb("dst_i", [P, TILES], I32)
        least = sb("least", [P, WINDOWS])
        most = sb("most", [P, WINDOWS])
        ends = sb("ends", [P, 2, nch])
        width = sb("width", [P, 2])
        diag = sb("diag", [P, nch, P])
        base_all = sb("base_all", [P, WINDOWS])
        ones = sb("ones", [P, P])
        fc2_in = sb("fc2_in", [P, WNUM])
        turned = [ctx.enter_context(nc.psum_tensor(f"turned{n}", [P, nch, P], F32)) for n in range(2)]
        spread = ctx.enter_context(nc.psum_tensor("spread", [P, 2 * BANK], F32))
        s_zero = sem("zeroed")
        s_ident = sem("ident_ready")
        s_w = sem("weights_in")
        s_dst = sem("dst_in")
        s_tab = sem("tables_in")
        s_ends = sem("window_ends_ready")
        s_turned = sem("ends_turned")
        s_diag = sem("diag_ready")
        s_spread = sem("bases_spread")
        s_width = sem("width_ready")
        s_wturned = sem("width_turned")
        s_chain = sem("vector_chain")
        block = ctx.enter_context(nc.Block())
        loads = []

        @block.sync
        def _(sp):
            sp.dma_start(dst_i[:, :], dst_t).then_inc(s_dst, 16)
            sp.wait_ge(s_zero, 4)
            wv, ws = k["wv"], k["ws"]
            to = [
                (k["fc1"][0:64, 0:64], fc_w1), (k["fc1"][64:128, 64:128], fc_w1),
                (fc2_in[0:64, :], fc_w2), (fc2_in[64:128, :], fc_w2),
                (k["l1s"][:, :], lin1_ws), (k["scs"][:, :], sc_ws),
                (ws[32:64, 0, :], lin2_ws[64:96, :]), (ws[96:128, 0, :], lin2_ws[64:96, :]),
                (ws[0:96, 1, :], lin2_ws[0:96, :]),
            ]
            for c in range(3):
                d = slice(NV * c, NV * c + NV)
                to += [(k["l1v"][d, d], lin1_wv), (k["scv"][d, d], sc_wv)]
                at = B_ROW[c]
                to += [(wv[at:at + 64, c, d], lin2_wv[0:64, :]),
                       (wv[NV * c:NV * c + NV, 3, d], lin2_wv[64:96, :])]
            to += [(wv[row:row + NV, c, NV * i:NV * i + NV], lin2_wv[96:128, :]) for c, row, i, _ in CROSS]
            for dst, of in to:
                sp.dma_start(dst, of).then_inc(s_w, 16)
            loads.append(len(to))
            sp.wait_ge(s_tab, 48)

        @block.scalar
        def _(act):
            act.dma_start(k["src"][:, :], src_t).then_inc(s_tab, 16)
            act.dma_start(k["ea"][:, :, :], ea_t).then_inc(s_tab, 16)
            act.dma_start(k["a"][:, :], a_t).then_inc(s_tab, 16)

        @block.gpsimd
        def _(pool):
            pool.memset(k["ident"][:, :], 0.0).then_inc(s_ident, 1)
            pool.wait_ge(s_ident, 1)
            pool.affine_select(out=k["ident"][:, :], in_=k["ident"][:, :], compare_op=ALU.not_equal,
                               fill=1.0, base=0, pattern=[[-1, P]], channel_multiplier=1)\
                .then_inc(s_ident, 1)
            pool.iota(k["iota"][:, :], pattern=[[1, SLOTS]], base=0, channel_multiplier=0,
                      allow_small_or_imprecise_dtypes=True).then_inc(s_ident, 1)
            pool.memset(ones[:, :], 1.0).then_inc(s_ident, 1)
            pool.memset(k["acc"][:, :, NODES_PAD:ACC_COLS], 0.0).then_inc(s_ident, 1)

        @block.vector
        def _(dve):
            for t in ("wv", "ws"):
                dve.memset(k[t][:, :, :], 0.0).then_inc(s_zero, 1)
            dve.memset(k["fc1"][:, :], 0.0).then_inc(s_zero, 1)
            dve.memset(k["l1v"][:, :], 0.0)
            dve.memset(k["scv"][:, :], 0.0).then_inc(s_zero, 1)
            dve.memset(ends[:, :, :], 0.0).then_inc(s_chain, 1)
            dve.wait_ge(s_dst, 16)
            dve.tensor_copy(k["rel"][:, :], dst_i[:, :]).then_inc(s_chain, 1)
            dve.wait_ge(s_chain, 2)
            by_window = k["rel"][:, :].rearrange("p (w t) -> p w t", t=TILES_W)
            dve.tensor_reduce(least[:, :], by_window, axis=AX.X, op=ALU.min).then_inc(s_ends, 1)
            dve.tensor_reduce(most[:, :], by_window, axis=AX.X, op=ALU.max).then_inc(s_ends, 1)
            dve.wait_ge(s_turned, 2)
            for n, op in ((0, ALU.min), (1, ALU.max)):
                for j, (_, m) in enumerate(chunks):
                    dve.tensor_reduce(ends[0:m, n, j:j + 1], turned[n][0:m, j, :], axis=AX.X, op=op)\
                       .then_inc(s_chain, 1)
            dve.wait_ge(s_chain, 2 + 2 * nch)
            dve.wait_ge(s_ident, 3)
            for j in range(nch):
                last = dve.tensor_scalar(diag[:, j, :], k["ident"][:, :], ends[:, 0, j:j + 1], None, ALU.mult)
                last.then_inc(s_diag, 1)
            dve.tensor_sub(ends[:, 1, :], ends[:, 1, :], ends[:, 0, :]).then_inc(s_chain, 1)
            dve.wait_ge(s_chain, 3 + 2 * nch)
            dve.tensor_reduce(width[:, 0:1], ends[:, 1, :], axis=AX.X, op=ALU.max).then_inc(s_width, 1)
            dve.wait_ge(s_spread, 1)
            dve.tensor_copy(base_all[:, :], spread[:, 0:WINDOWS]).then_inc(s_chain, 1)
            dve.memset(k["base"][:, 0:2], NODES_PAD)
            dve.wait_ge(s_chain, 4 + 2 * nch)
            dve.tensor_copy(k["base"][:, 2:2 + WINDOWS], base_all[0:1, :])
            dve.tensor_tensor(by_window, by_window,
                              base_all[:, :].unsqueeze(2).broadcast_to([P, WINDOWS, TILES_W]),
                              ALU.subtract)
            dve.wait_ge(s_wturned, 1)
            dve.tensor_reduce(width[0:1, 1:2], spread[0:1, 2 * BANK - P:2 * BANK], axis=AX.X, op=ALU.max)\
               .then_inc(s_chain, 1)
            dve.wait_ge(s_chain, 5 + 2 * nch)
            dve.tensor_copy(k["span"][:, :], width[0:1, 1:2])
            dve.wait_ge(s_w, 16 * loads[0])
            dve.tensor_scalar_mul(k["l1s"][:, :], k["l1s"][:, :], SC_S)
            dve.tensor_scalar_mul(k["l1v"][:, :], k["l1v"][:, :], SC_V)
            dve.tensor_scalar_mul(k["scs"][:, :], k["scs"][:, :], SC_S)
            dve.tensor_scalar_mul(k["scv"][:, :], k["scv"][:, :], SC_V)
            wv, ws = k["wv"], k["ws"]
            dve.tensor_scalar_mul(ws[:, :, :], ws[:, :, :], LIN2_S).then_inc(s_chain, 1)
            dve.tensor_scalar_mul(wv[:, :, :], wv[:, :, :], LIN2_V).then_inc(s_chain, 1)
            dve.wait_ge(s_chain, 7 + 2 * nch)
            dve.tensor_scalar_mul(ws[:, 0, :], ws[:, 0, :], 1.0 / math.sqrt(3.0))
            dve.tensor_scalar_mul(ws[64:96, 1, :], ws[64:96, 1, :], 1.0 / math.sqrt(3.0))
            for c, row, i, sign in CROSS:
                w = wv[row:row + NV, c, NV * i:NV * i + NV]
                dve.tensor_scalar_mul(w, w, sign / math.sqrt(2.0))
            dve.tensor_copy(k["fc2"][:, 0, :], fc2_in[:, :]).then_inc(s_chain, 1)
            dve.wait_ge(s_chain, 8 + 2 * nch)
            dve.tensor_sub(k["fc2"][:, 1, :], fc2_in[:, :], k["fc2"][:, 0, :].bitcast(F32))

        @block.tensor
        def _(pe):
            pe.wait_ge(s_ident, 2)
            for n, ends_of in enumerate((least, most)):
                pe.wait_ge(s_ends, n + 1)
                for j, (c, m) in enumerate(chunks):
                    last = pe.transpose(turned[n][0:m, j, :], ends_of[:, c:c + m], k["ident"][:, :])
                last.then_inc(s_turned, 1)
            pe.wait_ge(s_ident, 4)
            pe.wait_ge(s_diag, nch)
            for j, (c, m) in enumerate(chunks):
                last = pe.matmul(spread[:, c:c + m], ones[:, :], diag[:, j, 0:m], start=True, stop=True)
            last.then_inc(s_spread, 1)
            pe.wait_ge(s_width, 1)
            pe.wait_ge(s_chain, 4 + 2 * nch)
            pe.transpose(spread[0:1, 2 * BANK - P:2 * BANK], width[:, 0:1], k["ident"][:, :])\
              .then_inc(s_wturned, 1)


def warm_up(pe, k, ps):
    for _ in range(WARM_UP):
        pe.matmul(ps[:, :], k["ident"][:, :], k["rel"][:, 0:BANK], start=True, stop=True)


def node_stage(nc, k, x, table):
    TURN = 2 * GROUP
    x_v = x.rearrange("(t p) f -> p t f", p=P)
    table_v = table.rearrange("(t p) f -> p t f", p=P)
    with ExitStack() as ctx:
        def sb(name, shape, dt=F32):
            return ctx.enter_context(nc.sbuf_tensor(name, shape, dt))

        def sem(name):
            return ctx.enter_context(nc.semaphore(name))

        def pb(name):
            return [ctx.enter_context(nc.psum_tensor(f"{name}{n}", [P, BANK], F32)) for n in range(2)]

        xin = sb("xin", [P, TURN, FEAT])
        stats = sb("stats", [P, TURN, 6])
        mv = sb("mv", [P, TURN, 2])
        std = sb("std", [P, TURN])
        rstd = sb("rstd", [P, TURN])
        warm = sb("sqrt_table_loaded", [1, 1])
        shift = sb("shift", [P, TURN])
        h = sb("h", [P, TURN, FEAT])
        hts = sb("hts", [NS, 2, P])
        htv = sb("htv", [VEC, 2, P])
        rows = sb("rows", [P, TURN, FEAT])
        ps_ts, ps_tv = pb("scalars_turned"), pb("vectors_turned")
        ps_r, ps_s = pb("node_rows"), pb("node_self")
        x_in = [sem(f"x_in{c}") for c in range(len(LOADS))]
        stats_ok = sem("stats_ready")
        stats_seen = sem("stats_seen")
        mv_ok = sem("mean_var_ready")
        var_ok = sem("var_ready")
        std_ok = sem("std_ready")
        rstd_ok = sem("rstd_ready")
        shift_ok = sem("shift_ready")
        h_ok = sem("h_ready")
        turned = sem("h_turned")
        hts_ok, htv_ok = sem("hT_scalars_ready"), sem("hT_vectors_ready")
        lin_ok = sem("linear1_done")
        rows_ok = sem("rows_ready")
        self_ok = sem("self_kept")
        out_done = [sem(f"rows_out{g}") for g in range(2)]
        rows_free = [sem(f"rows_free{g}") for g in range(2)]
        block = ctx.enter_context(nc.Block())

        def turns(engine, body):
            with engine.Fori(0, NODE_ITERS - 1) as i:
                body(i, 2 * TURN)
            body(NODE_ITERS - 1, TURN)

        def load(sp, turn, c):
            lo, hi = LOADS[c]
            sp.dma_start(xin[:, lo:hi, :], x_v[:, bass.ds(turn * TURN + lo, hi - lo), :]).then_inc(x_in[c], 16)

        @block.sync
        def _(sp):
            for c in range(len(LOADS)):
                load(sp, 0, c)
            with sp.Fori(0, NODE_ITERS - 1) as i:
                for c in range(len(LOADS)):
                    sp.wait_ge(h_ok, i * TURN + LOADS[c][1])
                    load(sp, i + 1, c)

        @block.gpsimd
        def _(pool):
            def store(i, g):
                pool.wait_ge(rows_ok, i * TURN + (g + 1) * GROUP + 2)
                pool.dma_start(table_v[:, bass.ds(i * TURN + g * GROUP, GROUP), :],
                               rows[:, g * GROUP:(g + 1) * GROUP, :]).then_inc(out_done[g], 16)

            for g in range(2):
                pool.sem_inc(rows_free[g], 1)
            with pool.Fori(0, NODE_ITERS) as i:
                for g in range(2):
                    store(i, g)
                    pool.wait_ge(out_done[g], 16 * i + 16)
                    pool.sem_inc(rows_free[g], 1)

        @block.vector
        def _(dve):
            def stat(i, t):
                for c, (lo, _) in enumerate(LOADS):
                    if t % TURN == lo:
                        dve.wait_ge(x_in[c], 16 * (i + t // TURN) + 16)
                dve.bn_stats(stats[:, t % TURN, :], xin[:, t % TURN, :]).then_inc(stats_ok, 1)

            def mean_var(i, t):
                dve.wait_ge(stats_ok, i * TURN + t + GROUP)
                dve.sem_inc(stats_seen, 1)
                for n in range(t, t + GROUP):
                    dve.bn_aggr(mv[:, n % TURN, :], stats[:, n % TURN, :]).then_inc(mv_ok, 1)

                grp = slice(t % TURN, t % TURN + GROUP)
                dve.wait_ge(mv_ok, i * TURN + t + GROUP)
                dve.tensor_scalar_add(std[:, grp], mv[:, grp, 1], 1e-5).then_inc(var_ok, 1)

            def normal(i, t):
                grp = slice(t % TURN, t % TURN + GROUP)
                dve.wait_ge(std_ok, 2 * i + t // GROUP + 1)
                dve.reciprocal(rstd[:, grp], std[:, grp]).then_inc(rstd_ok, 1)
                dve.wait_ge(rstd_ok, 2 * i + t // GROUP + 1)
                dve.scalar_tensor_tensor(out=shift[:, grp], in0=mv[:, grp, 0], scalar=-1.0,
                                         in1=rstd[:, grp], op0=ALU.mult, op1=ALU.mult)\
                   .then_inc(shift_ok, 1)

            def row(i, t):
                if t % GROUP == 0:
                    dve.wait_ge(rows_free[t // GROUP], i + 1)
                dve.wait_ge(lin_ok, i * TURN + t + 1)
                dve.tensor_scalar(rows[:, t, :], ps_r[t % 2][:, 0:FEAT],
                                  k["a"][:, bass.ds(i * TURN + t, 1)], None, ALU.mult)\
                   .then_inc(rows_ok, 1)

            def body(i, until):
                for t in range(TURN):
                    dve.wait_ge(turned, i * TURN + t + 1)
                    dve.tensor_copy(hts[:, t % 2, :], ps_ts[t % 2][0:NS, 0:P]).then_inc(hts_ok, 1)
                    half = t // GROUP * GROUP + GROUP
                    at = t % GROUP
                    if half < until:
                        for n in ((0, 1), (2, 3), (4, 5), (6,))[at] if at < 4 else ():
                            stat(i, half + n)
                    if t:
                        row(i, t - 1)
                    if half < until:
                        if at == 3:
                            mean_var(i, half)
                        if at == 4:
                            normal(i, half)
                row(i, TURN - 1)

            dve.sem_inc(rows_ok, 2)
            for t in range(GROUP):
                stat(0, t)
            mean_var(0, 0)
            normal(0, 0)
            turns(dve, body)

        @block.scalar
        def _(act):
            def relu(i, t):
                if t % GROUP == 0:
                    act.wait_ge(shift_ok, 2 * i + t // GROUP + 1)
                n = t % TURN
                act.activation(h[:, n, :], xin[:, n, :], ACT.Relu, bias=shift[:, n:n + 1],
                               scale=rstd[:, n:n + 1]).then_inc(h_ok, 1)

            def keep(i, t):
                act.wait_ge(lin_ok, i * TURN + t + 1)
                act.activation(k["acc"][:, :, bass.ds((i * TURN + t) * P, P)],
                               ps_s[t % 2][0:OUTS, 0:2 * P].rearrange("p (a n) -> p a n", a=2),
                               ACT.Copy).then_inc(self_ok, 1)

            def root(i, t):
                grp = slice(t % TURN, t % TURN + GROUP)
                act.wait_ge(var_ok, 2 * i + t // GROUP + 1)
                act.activation(std[:, grp], std[:, grp], ACT.Sqrt).then_inc(std_ok, 1)

            def body(i, until):
                act.activation(warm[:, :], k["ident"][0:1, 0:1], ACT.Sqrt)
                for t in range(TURN):
                    act.wait_ge(turned, i * TURN + t + 1)
                    act.activation(htv[:, t % 2, :], ps_tv[t % 2][0:VEC, 0:P], ACT.Copy).then_inc(htv_ok, 1)
                    if t + 2 < until:
                        relu(i, t + 2)
                    if t:
                        keep(i, t - 1)
                    half = t // GROUP * GROUP + GROUP
                    if half < until and t % GROUP == 3:
                        root(i, half)
                keep(i, TURN - 1)

            act.sem_inc(self_ok, 2)
            root(0, 0)
            relu(0, 0)
            relu(0, 1)
            turns(act, body)

        @block.tensor
        def _(pe):
            def turn(i, t):
                pe.wait_ge(h_ok, i * TURN + t + 1)
                pe.transpose(ps_tv[t % 2][0:VEC, 0:P], h[:, t % TURN, NS:FEAT], k["ident"][:, :])
                pe.transpose(ps_ts[t % 2][0:NS, 0:P], h[:, t % TURN, 0:NS], k["ident"][:, :])\
                  .then_inc(turned, 1)

            def body(i, until):
                for t in range(TURN):
                    if t + 1 < until:
                        turn(i, t + 1)
                    hs, hv = hts[:, t % 2, :], htv[:, t % 2, :]
                    pe.wait_ge(rows_ok, i * TURN + t + 1)
                    pe.wait_ge(hts_ok, i * TURN + t + 1)
                    pe.matmul(ps_r[t % 2][:, 0:NS], hs, k["l1s"][:, :], start=True, stop=True)
                    pe.wait_ge(htv_ok, i * TURN + t + 1)
                    pe.matmul(ps_r[t % 2][:, NS:FEAT], hv, k["l1v"][:, :], start=True, stop=True)
                    pe.wait_ge(self_ok, i * TURN + t + 1)
                    pe.matmul(ps_s[t % 2][0:OUTS, 0:P], k["scv"][:, :], hv, start=True, stop=True)
                    pe.matmul(ps_s[t % 2][0:OUTS, P:2 * P], k["scs"][:, :], hs, start=True, stop=True)\
                      .then_inc(lin_ok, 1)

            warm_up(pe, k, ps_r[0])
            turn(0, 0)
            turns(pe, body)


def edge_buffers(nc, ctx):
    def sb(name, shape, dt=F32):
        return ctx.enter_context(nc.sbuf_tensor(name, shape, dt))

    def pb(name, banks=1):
        return ctx.enter_context(nc.psum_tensor(name, [P, banks * BANK], F32))

    def sem(name):
        return ctx.enter_context(nc.semaphore(name))

    return dict(
        idx=sb("idx", [P, 2, STEP_TILES], I32),
        rows=sb("gathered", [P, 2, STEP_TILES, FEAT]),
        est=sb("edge_scalars", [P, 2, PAIRS * P]),
        hid=sb("hidden", [P, 2, PAIRS * P]),
        hid2=sb("hidden_parts", [P, 2, 2, PAIRS * P], F32R),
        hot=sb("onehot", [P, STEP_TILES, SLOTS]),
        s=sb("weighted_onehot", [P, 2, STEP_TILES, 4, SLOTS]),
        msg=sb("messages", [P, PAIRS, 2, MSG]),
        sums=sb("sums", [P, 2, SUMS]),
        turned=sb("sums_turned", [P, 2, 3, P]),
        zeros=sb("zeros", [P, 3 * P]),
        w_ps=[pb(f"weights_ps{p}") for p in range(PAIRS)], sum_ps=[pb("sums_ps_a"), pb("sums_ps_b")],
        hid_ps=pb("hidden_ps"), turn_ps=pb("turned_ps"), out_ps=pb("out_ps"),
        zeroed=sem("zeros_ready"), 
        est_in=[sem(f"edge_scalars_in{u}") for u in range(2)],
        idx_ok=sem("indices_ready"), gathers_begun=sem("gathers_begun"),
        rows_in=[sem(f"rows_gathered{u}") for u in range(2)],
        hid_mm=sem("hidden_product_done"), hid_ok=sem("hidden_ready"),
        split_ok=sem("hidden_split"),
        w_mm=sem("weights_done"),
        hot_ok=sem("onehot_ready"), s_ok=sem("weighted_onehot_ready"), s_act_ok=sem("weighted_onehot_scalar_ready"),
        msg_ok=sem("messages_ready"),
        sum_mm=sem("window_summed"), sum_ok=sem("sums_copied"),
        turn_mm=sem("sums_turned_ps"), turn_ok=sem("sums_turned_copied"),
        out_mm=sem("linear2_done"), out_added=sem("window_added"),
    )


EDGE_SEMS = ("zeroed", "est_in", "idx_ok", "gathers_begun", "rows_in", "hid_mm", "hid_ok",
             "split_ok", "w_mm", "hot_ok", "s_ok", "s_act_ok", "msg_ok", "sum_mm", "sum_ok", "turn_mm", "turn_ok", "out_mm", "out_added")


def edge_pass(nc, k, b, table, es_t, name):
    with ExitStack() as ctx:
        block = ctx.enter_context(nc.Block(name=f"edges_{name}"))

        def load_scalars(sp, step, u):
            sp.dma_start(b["est"][:, u, :], es_t[bass.ds(step, 1), :, :].rearrange("s p e -> p (s e)"))\
              .then_inc(b["est_in"][u], 16)

        @block.sync
        def _(sp):
            for u in range(2):
                load_scalars(sp, u, u)
            with sp.Fori(0, ITERS - 1) as i:
                for u in range(2):
                    sp.wait_ge(b["hid_mm"], 2 * i + u + 1)
                    load_scalars(sp, 2 * i + 2 + u, u)
            sp.wait_ge(b["hid_mm"], STEPS - 1)
            load_scalars(sp, STEPS, 0)
            sp.wait_ge(b["est_in"][0], 16 * (ITERS + 1))

        @block.gpsimd
        def _(pool):
            pool.memset(b["zeros"][:, :], 0.0).then_inc(b["zeroed"], 1)

            def gather(step, u, nth):
                pool.tensor_copy(b["idx"][:, u, :], k["src"][:, bass.ds(step * STEP_TILES, STEP_TILES)])\
                    .then_inc(b["idx_ok"], 1)
                pool.wait_ge(b["idx_ok"], nth)
                pool.sem_inc(b["gathers_begun"], 1)
                for t in range(STEP_TILES):
                    pool.indirect_dma_start(
                        b["rows"][:, u, t, :], None, table[:, :],
                        bass.IndirectOffsetOnAxis(ap=b["idx"][:, u, t:t + 1], axis=0))\
                        .then_inc(b["rows_in"][u], 16)

            for u in range(2):
                gather(u, u, u + 1)
            with pool.Fori(0, ITERS - 1) as i:
                for u in range(2):
                    pool.wait_ge(b["msg_ok"], (2 * i + u) * PAIRS + PAIRS)
                    gather(2 * i + 2 + u, u, 2 * i + u + 3)
            for u in range(2):
                pool.wait_ge(b["rows_in"][u], ITERS * 16 * STEP_TILES)

        @block.scalar
        def _(act):
            def hidden(u, n):
                act.wait_ge(b["hid_mm"], n)
                scale = 1.0 / math.sqrt(64.0)
                ps = b["hid_ps"][:, 0:PAIRS * P]
                act.activation(b["hid2"][0:64, u, 0, :], ps[0:64, :], ACT.Silu, scale=scale)
                act.activation(b["hid2"][64:128, u, 1, :], ps[64:128, :], ACT.Silu, scale=scale)
                act.activation(b["hid"][:, u, :], ps, ACT.Silu, scale=scale).then_inc(b["hid_ok"], 1)

            def copy_sums(half, window):
                act.wait_ge(b["sum_mm"], window + 1)
                act.activation(b["sums"][:, half, :], b["sum_ps"][half][:, 0:SUMS], ACT.Copy)\
                   .then_inc(b["sum_ok"], 1)

            def copy_turned(half, flush):
                act.wait_ge(b["turn_mm"], flush)
                act.activation(b["turned"][:, half, :, :],
                               b["turn_ps"][:, 0:3 * P].rearrange("p (a n) -> p a n", a=3), ACT.Copy)\
                   .then_inc(b["turn_ok"], 1)

            def weigh(step, u):
                act.wait_ge(b["hot_ok"], step + 1)
                for t in range(STEP_TILES - 2, STEP_TILES):
                    for c in range(4):
                        last = act.activation(
                            b["s"][:, u, t, c, :], b["hot"][:, t, :], ACT.Copy,
                            scale=k["ea"][:, bass.ds(step * STEP_TILES + t, 1), c])
                last.then_inc(b["s_act_ok"], 1)

            act.wait_ge(b["zeroed"], 1)
            act.activation(b["turned"][:, 0, :, :],
                           b["zeros"][:, :].rearrange("p (a n) -> p a n", a=3), ACT.Copy)\
               .then_inc(b["turn_ok"], 1)
            act.activation(b["sums"][:, 1, :], b["zeros"][:, 0:SUMS], ACT.Copy)\
               .then_inc(b["sum_ok"], 1)
            hidden(0, 1)
            weigh(0, 0)
            with act.Fori(0, ITERS) as i:
                for u in range(2):
                    step = 2 * i + u
                    hidden(1 - u, step + 2)
                    copy_turned(1, 2 * step + 1)
                    copy_sums(0, 2 * step)
                    weigh(step + 1, 1 - u)
                    copy_turned(0, 2 * step + 2)
                    copy_sums(1, 2 * step + 1)
            copy_turned(1, 2 * STEPS + 1)

        @block.vector
        def _(dve):
            def onehots(step):
                dve.tensor_tensor(
                    b["hot"][:, :, :],
                    k["iota"][:, :].unsqueeze(1).broadcast_to([P, STEP_TILES, SLOTS]),
                    k["rel"][:, bass.ds(step * STEP_TILES, STEP_TILES)].unsqueeze(2)
                    .broadcast_to([P, STEP_TILES, SLOTS]), ALU.is_equal).then_inc(b["hot_ok"], 1)

            def weigh(step, u, p):
                dve.wait_ge(b["hot_ok"], step + 1)
                dve.tensor_tensor(
                    b["s"][:, u, 2 * p:2 * p + 2, :, :],
                    b["hot"][:, 2 * p:2 * p + 2, :].unsqueeze(2).broadcast_to([P, 2, 4, SLOTS]),
                    k["ea"][:, bass.ds(step * STEP_TILES + 2 * p, 2), :].unsqueeze(3)
                    .broadcast_to([P, 2, 4, SLOTS]), ALU.mult).then_inc(b["s_ok"], 1)

            def messages(u, p, pair):
                dve.wait_ge(b["w_mm"], pair + 1)
                m = b["msg"][:, p, :, :]
                w = b["w_ps"][p][:, 0:2 * WNUM].rearrange("p (t c) -> p t c", t=2)
                g = b["rows"][:, u, 2 * p:2 * p + 2, :]

                def blocks(v, at, count, stride, width):
                    near = v[:, :, at // stride * stride:at // stride * stride + count * stride]
                    off = at % stride
                    return near.rearrange("p t (k c) -> p t k c", k=count)[:, :, :, off:off + width]

                dve.tensor_tensor(
                    blocks(m, M_A, 2, M_B - M_A, NS), blocks(w, W_AB, 2, NS, NS),
                    g[:, :, 0:NS].unsqueeze(2).broadcast_to([P, 2, 2, NS]), ALU.mult)
                for at, of, first, n in ((M_C, W_C, 0, 3), (M_DX, W_D, 0, 2), (M_FY, W_F, 1, 2),
                                         (M_DZ, W_D, 2, 1), (M_FX, W_F, 0, 1)):
                    last = dve.tensor_tensor(
                        blocks(m, at, n, NV, NV), w[:, :, of:of + NV].unsqueeze(2).broadcast_to([P, 2, n, NV]),
                        blocks(g, NS + NV * first, n, NV, NV), ALU.mult)
                last.then_inc(b["msg_ok"], 1)

            def split(u, nth):
                dve.wait_ge(b["hid_ok"], nth)
                for t, first, second in ((0, slice(0, 64), slice(64, 128)), (1, slice(64, 128), slice(0, 64))):
                    last = dve.tensor_sub(b["hid2"][second, u, t, :], b["hid"][first, u, :],
                                          b["hid2"][first, u, t, :].bitcast(F32))
                last.then_inc(b["split_ok"], 1)

            def add(half, base):
                a = k["acc"][:, :, bass.ds(base, SLOTS)]
                out = b["out_ps"][0:OUTS, 0:2 * P].rearrange("p (a n) -> p a n", a=2)
                dve.tensor_tensor(a, a, out[:, :, half * SLOTS:(half + 1) * SLOTS], ALU.add)\
                   .then_inc(b["out_added"], 1)

            def bases(first, n):
                return nc.values_load_multi_w_load_instructions(
                    k["base"][0:1, bass.ds(first, n)], engines=(mybir.EngineType.DVE,), min_val=0,
                    max_val=NODES_PAD, skip_runtime_bounds_check_because="least dst, or the pad")[1]

            for ps in b["sum_ps"]:
                dve.memset(ps[0:64, SUM_GAP:SUM_Z], 0.0)
            onehots(0)
            for p in range(PAIRS - 1):
                weigh(0, 0, p)
            split(0, 1)
            with dve.Fori(0, ITERS) as i:
                for u in range(2):
                    step = 2 * i + u
                    pair = PAIRS * step
                    dve.wait_ge(b["rows_in"][u], (i + 1) * 16 * STEP_TILES)
                    messages(u, 0, pair)
                    if u == 0:
                        at = bases(4 * i, 4)
                    dve.wait_ge(b["s_ok"], (PAIRS - 1) * (step + 1))
                    dve.wait_ge(b["s_act_ok"], step + 1)
                    onehots(step + 1)
                    messages(u, 1, pair + 1)
                    weigh(step + 1, 1 - u, 0)
                    split(1 - u, step + 2)
                    messages(u, 2, pair + 2)
                    dve.wait_ge(b["out_mm"], step + 1)
                    add(0, at[2 * u])
                    weigh(step + 1, 1 - u, 1)
                    dve.wait_ge(b["out_added"], 2 * step + 1)
                    add(1, at[2 * u + 1])
            at = bases(2 * STEPS, 2)
            dve.wait_ge(b["out_mm"], STEPS + 1)
            add(0, at[0])
            dve.wait_ge(b["out_added"], 2 * STEPS + 1)
            add(1, at[1])

        @block.tensor
        def _(pe):
            def hidden(u, nth):
                pe.wait_ge(b["est_in"][u], 16 * nth)
                pe.matmul(b["hid_ps"][:, 0:PAIRS * P], k["fc1"][:, :], b["est"][:, u, :],
                          start=True, stop=True).then_inc(b["hid_mm"], 1)

            def weights(u, p):
                for t in range(2):
                    for part in range(2):
                        last = pe.matmul(b["w_ps"][p][:, t * WNUM:(t + 1) * WNUM],
                                         b["hid2"][:, u, t, p * P:(p + 1) * P], k["fc2"][:, part, :],
                                         start=part == 0, stop=part == 1)
                last.then_inc(b["w_mm"], 1)

            def sum_tile(u, t):
                first, end = t % TILES_W == 0, t % TILES_W == TILES_W - 1
                ps = b["sum_ps"][t // TILES_W]
                m = b["msg"][:, t // 2, t % 2, :]
                s0, sx, sy, sz = (b["s"][:, u, t, c, :] for c in range(4))
                run = M_B - M_FY
                y_runs = m[:, M_FY:M_FY + 2 * run].rearrange("p (k c) -> p k c", k=2)[:, :, 0:3 * NV]
                lo, hi = ps[0:64, :], ps[64:128, :]
                for out, lhs, rhs, start, stop in (
                    (hi[:, SUM_0:SUM_0 + 5 * NV], s0, m[:, M_C:M_C + 5 * NV], first, end),
                    (lo[:, SUM_Z:SUM_Z + 5 * NV], sz, m[:, M_FZ:M_FZ + 5 * NV], first, end),
                    (hi[:, SUM_Y:SUM_Y + 6 * NV].rearrange("p (k c) -> p k c", k=2), sy, y_runs, False, end),
                    (lo[:, SUM_X:SUM_X + 5 * NV], sx, m[:, M_DY:M_DY + 5 * NV], False, end),
                ):
                    last = pe.matmul(out, lhs, rhs, start=start, stop=stop, skip_group_check=True)
                return last

            def turn(half):
                sums = b["sums"][:, half, :]
                for n, c in enumerate(TURNED_AT):
                    last = pe.transpose(b["turn_ps"][:, n * P:(n + 1) * P], sums[:, c:c + P], k["ident"][:, :])
                last.then_inc(b["turn_mm"], 1)

            def linear2():
                def piece(n, half):
                    return b["turned"][:, :, n, half * SLOTS:(half + 1) * SLOTS]

                out = b["out_ps"][0:OUTS, :]
                wv, ws = k["wv"], k["ws"]
                vec = [(wv[:, 0, :], piece(0, 0)), (wv[:, 3, :], piece(0, 1)),
                       (wv[:, 2, :], piece(1, 0)), (wv[:, 1, :], piece(1, 1))]
                sca = [(ws[:, 0, :], piece(2, 0)), (ws[:, 1, :], piece(2, 1))]
                for n, (w, r) in enumerate(vec):
                    pe.matmul(out[:, 0:P], w, r, start=n == 0, stop=n == len(vec) - 1)
                for n, (w, r) in enumerate(sca):
                    last = pe.matmul(out[:, P:2 * P], w, r, start=n == 0, stop=n == len(sca) - 1)
                last.then_inc(b["out_mm"], 1)

            hidden(0, 1)
            pe.wait_ge(b["split_ok"], 1)
            weights(0, 0)
            weights(0, 1)
            with pe.Fori(0, ITERS) as i:
                for u in range(2):
                    step = 2 * i + u
                    pe.wait_ge(b["msg_ok"], PAIRS * step + 1)
                    hidden(1 - u, i + 1 + u)
                    sum_tile(u, 0)
                    pe.wait_ge(b["turn_ok"], 2 * step + 1)
                    pe.wait_ge(b["sum_ok"], 2 * step + 1)
                    turn(1)
                    sum_tile(u, 1)
                    weights(u, 2)
                    pe.wait_ge(b["msg_ok"], PAIRS * step + 2)
                    sum_tile(u, 2).then_inc(b["sum_mm"], 1)
                    pe.wait_ge(b["turn_ok"], 2 * step + 2)
                    linear2()
                    sum_tile(u, 3)
                    pe.wait_ge(b["split_ok"], step + 2)
                    weights(1 - u, 0)
                    pe.wait_ge(b["msg_ok"], PAIRS * step + 3)
                    pe.wait_ge(b["s_act_ok"], step + 1)
                    sum_tile(u, 4)
                    pe.wait_ge(b["sum_ok"], 2 * step + 2)
                    turn(0)
                    sum_tile(u, 5).then_inc(b["sum_mm"], 1)
                    weights(1 - u, 1)
            pe.wait_ge(b["turn_ok"], 2 * STEPS + 1)
            pe.wait_ge(b["sum_ok"], 2 * STEPS + 1)
            turn(1)
            pe.wait_ge(b["turn_ok"], 2 * STEPS + 2)
            pe.wait_ge(b["out_added"], 2 * STEPS)
            linear2()


def further_passes(nc, k, b, table, es_t):
    def widest():
        return nc.values_load(k["span"][0:1, 0:1], min_val=0, max_val=NODES - 1,
                              skip_runtime_bounds_check_because="a difference of two dst")

    with nc.If(widest() >= SLOTS):
        with nc.Fori(1, PASSES):
            with nc.If(widest() >= SLOTS):
                nc.all_engine_barrier()
                with ExitStack() as ctx:
                    block = ctx.enter_context(nc.Block(name="move_windows"))

                    @block.vector
                    def _(dve):
                        dve.tensor_scalar_add(k["rel"][:, :], k["rel"][:, :], -float(SLOTS))
                        dve.tensor_scalar_add(k["span"][:, :], k["span"][:, :], -float(SLOTS))
                        dve.tensor_scalar(k["base"][:, :], k["base"][:, :], float(SLOTS), float(NODES_PAD),
                                          ALU.add, ALU.min)

                    @block.gpsimd
                    def _(pool):
                        for s in b["rows_in"]:
                            pool.dma_reset(range(s.num, s.num + 1))
                        for name in EDGE_SEMS:
                            sems = b[name] if isinstance(b[name], list) else [b[name]]
                            for s in sems:
                                pool.sem_clear(s)
                edge_pass(nc, k, b, table, es_t, "further")


def finish_stage(nc, k, x, y):
    TURN = 2 * GROUP
    x_v = x.rearrange("(t p) f -> p t f", p=P)
    y_v = y.rearrange("(t p) f -> p t f", p=P)
    with ExitStack() as ctx:
        def sb(name, shape, dt=F32):
            return ctx.enter_context(nc.sbuf_tensor(name, shape, dt))

        def sem(name):
            return ctx.enter_context(nc.semaphore(name))

        xin = sb("x_again", [P, TURN, FEAT])
        part = sb("acc_part", [OUTS, GROUP, 2, P])
        sig = sb("sigmoid", [P, GROUP, OUTS])
        out = sb("out_rows", [P, TURN, FEAT])
        ps = [ctx.enter_context(nc.psum_tensor(f"pre_ps{n}", [P, BANK], F32)) for n in range(GROUP)]
        x_in = [sem(f"x_again_in{c}") for c in range(len(LOADS))]
        part_ok = sem("part_ready")
        pre_ok = sem("pre_ready")
        sig_ok = sem("sigmoid_ready")
        gated_ok = sem("gated_ready")
        rows_ok = sem("out_rows_ready")
        out_done = [sem(f"out_done{g}") for g in range(2)]
        rows_free = [sem(f"out_rows_free{g}") for g in range(2)]
        block = ctx.enter_context(nc.Block())

        def load(sp, turn, c):
            lo, hi = LOADS[c]
            sp.dma_start(xin[:, lo:hi, :], x_v[:, bass.ds(turn * TURN + lo, hi - lo), :]).then_inc(x_in[c], 16)

        @block.sync
        def _(sp):
            for c in range(len(LOADS)):
                load(sp, 0, c)
            with sp.Fori(0, NODE_ITERS - 1) as i:
                for c, (_, hi) in enumerate(LOADS):
                    sp.wait_ge(rows_ok, i * TURN + hi)
                    load(sp, i + 1, c)

        @block.gpsimd
        def _(pool):
            def store(i, g):
                pool.wait_ge(rows_ok, i * TURN + (g + 1) * GROUP)
                pool.dma_start(y_v[:, bass.ds(i * TURN + g * GROUP, GROUP), :],
                               out[:, g * GROUP:(g + 1) * GROUP, :]).then_inc(out_done[g], 16)

            for g in range(2):
                pool.sem_inc(rows_free[g], 1)
            with pool.Fori(0, NODE_ITERS) as i:
                for g in range(2):
                    store(i, g)
                    pool.wait_ge(out_done[g], 16 * i + 16)
                    pool.sem_inc(rows_free[g], 1)

        @block.scalar
        def _(act):
            def part_of(i, t):
                act.activation(part[:, t % GROUP, :, :], k["acc"][:, :, bass.ds((i * TURN + t) * P, P)],
                               ACT.Copy).then_inc(part_ok, 1)

            def body(i, until):
                for t in range(TURN):
                    act.wait_ge(pre_ok, i * TURN + t + 1)
                    act.activation(sig[:, t % GROUP, :], ps[t % GROUP][:, OUTS:2 * OUTS], ACT.Sigmoid,
                                   scale=k["a"][:, bass.ds(i * TURN + t, 1)]).then_inc(sig_ok, 1)
                    if t + 3 < until:
                        part_of(i, t + 3)

            for t in range(3):
                part_of(0, t)
            with act.Fori(0, NODE_ITERS - 1) as i:
                body(i, 2 * TURN)
            body(NODE_ITERS - 1, TURN)

        @block.tensor
        def _(pe):
            with pe.Fori(0, NODE_ITERS) as i:
                for t in range(TURN):
                    pe.wait_ge(part_ok, i * TURN + t + 1)
                    pe.wait_ge(gated_ok, i * TURN + t + 1)
                    for n in range(2):
                        last = pe.transpose(ps[t % GROUP][:, n * OUTS:(n + 1) * OUTS],
                                            part[:, t % GROUP, n, :], k["ident"][0:OUTS, 0:OUTS])
                    last.then_inc(pre_ok, 1)

        @block.vector
        def _(dve):
            def gate(i, t):
                if t % GROUP == 0:
                    dve.wait_ge(rows_free[t // GROUP], i + 1)
                a = k["a"][:, bass.ds(i * TURN + t, 1)]
                n = t % GROUP
                dve.wait_ge(sig_ok, i * TURN + t + 1)
                dve.scalar_tensor_tensor(out=out[:, t, 0:NS], in0=ps[n][:, OUTS:OUTS + NS],
                                         scalar=a, in1=sig[:, n, 0:NS], op0=ALU.mult, op1=ALU.mult)
                dve.scalar_tensor_tensor(
                    out=out[:, t, NS:FEAT].rearrange("p (i c) -> p i c", i=3),
                    in0=ps[n][:, 0:VEC].rearrange("p (i c) -> p i c", i=3), scalar=a,
                    in1=sig[:, n, NS:OUTS].unsqueeze(1).broadcast_to([P, 3, NV]),
                    op0=ALU.mult, op1=ALU.mult).then_inc(gated_ok, 1)

            def add_x(i, t):
                for c, (lo, _) in enumerate(LOADS):
                    if t == lo:
                        dve.wait_ge(x_in[c], 16 * i + 16)
                dve.wait_ge(gated_ok, i * TURN + t + 1 + GROUP)
                dve.tensor_add(out[:, t, :], out[:, t, :], xin[:, t, :]).then_inc(rows_ok, 1)

            dve.sem_inc(gated_ok, GROUP)
            with dve.Fori(0, NODE_ITERS) as i:
                for t in range(TURN):
                    gate(i, t)
                    if t:
                        add_x(i, t - 1)
                add_x(i, TURN - 1)


def kernel(x, src, dst, edge_attr_4, edge_attr_64, node_vec1, L0_gnn_lin1_ws, L0_gnn_lin1_wv,
           L0_gnn_fc_w1, L0_gnn_fc_w2, L0_gnn_sc_ws, L0_gnn_sc_wv, L0_gnn_lin2_ws, L0_gnn_lin2_wv):
    import numpy as np
    import concourse.bacc as bacc
    from concourse.bass_utils import run_bass_kernel_spmd

    x = np.asarray(x)
    nodes = np.zeros((NODES_PAD, FEAT), np.float32)
    nodes[:NODES, :NS] = x[:, :NS]
    nodes[:NODES, NS:] = x[:, NS:].reshape(NODES, NV, 3).transpose(0, 2, 1).reshape(NODES, VEC)
    attr = np.zeros((NODES_PAD,), np.float32)
    attr[:NODES] = np.asarray(node_vec1)[:, 0]
    more = TILES * P - EDGES
    tiled = lambda v: np.ascontiguousarray(v.reshape(TILES, P).T)
    scalars = np.zeros((STEPS + 1, PAIRS, 2, P, NS), np.float32)
    scalars.reshape(-1, NS)[:EDGES] = np.asarray(edge_attr_64)
    ea = np.pad(np.asarray(edge_attr_4), ((0, more), (0, 0)))
    arrays = dict(
        x=nodes, node_attr=np.ascontiguousarray(attr.reshape(NODE_TILES, P).T),
        src=tiled(np.pad(np.asarray(src), (0, more))),
        dst=tiled(np.pad(np.asarray(dst), (0, more), mode="edge")),
        edge_attr=np.ascontiguousarray(ea.reshape(TILES, P, 4).transpose(1, 0, 2)),
        edge_scalars=np.ascontiguousarray(scalars.transpose(0, 2, 4, 1, 3).reshape(STEPS + 1, P, PAIRS * P)),
        lin1_ws=L0_gnn_lin1_ws, lin1_wv=L0_gnn_lin1_wv, fc_w1=L0_gnn_fc_w1, fc_w2=L0_gnn_fc_w2,
        sc_ws=L0_gnn_sc_ws, sc_wv=L0_gnn_sc_wv, lin2_ws=L0_gnn_lin2_ws, lin2_wv=L0_gnn_lin2_wv)
    arrays = {f"in_{n}": np.ascontiguousarray(v) for n, v in arrays.items()}

    nc = bacc.Bacc("TRN2", target_bir_lowering=False, num_devices=1)
    args = [nc.dram_tensor(n, v.shape, mybir.dt.from_np(v.dtype), kind="ExternalInput").ap()
            for n, v in arrays.items()]
    args.append(nc.dram_tensor("y", (NODES_PAD, FEAT), F32, kind="ExternalOutput").ap())
    build(nc, *args)
    got = np.asarray(run_bass_kernel_spmd(nc, [arrays], core_ids=[0]).results[0]["y"])[:NODES]
    out = np.empty((NODES, FEAT), np.float32)
    out[:, :NS] = got[:, :NS]
    out[:, NS:] = got[:, NS:].reshape(NODES, 3, NV).transpose(0, 2, 1).reshape(NODES, VEC)
    return out
```
